# Optimizing a Trainium2 kernel written in Bass

```python
import numpy as np
import jax
import jax.numpy as jnp

def _softmax(x, axis=-1):
    return jax.nn.softmax(x, axis=axis)

def _gelu(x):
    return jax.nn.gelu(x, approximate=True)

def _silu(x):
    return jax.nn.silu(x)

def _sigmoid(x):
    return jax.nn.sigmoid(x)

def _layernorm(x, axis=-1, eps=1e-05):
    m = jnp.mean(x, axis=axis, keepdims=True)
    v = jnp.var(x, axis=axis, keepdims=True)
    return (x - m) / jnp.sqrt(v + eps)

def _scatter_add(tgt, idx, src, axis=0):
    return tgt.at[idx].add(src)

def _segment_sum(src, seg, n):
    return jax.ops.segment_sum(src, seg, n)
kernel_name = 'mk_conv_preact_d2_conv_nhwc768_r2_94e408'

def setup_inputs(seed: int=0):
    np.random.seed(seed)
    _w = jnp.asarray

    def _rec_inputs():
        import jax
        import jax.numpy as jnp
        _gk = jax.random.key(seed)
        x = -0.0004039 + 1 * jax.random.normal(jax.random.fold_in(_gk, 1), (4, 32, 32, 384), jnp.float32)
        return x
    x = _rec_inputs()

    def _L0_conv_setup():
        import jax, jax.numpy as jnp
        import numpy as np
        B_, H_, W_, DM = (4, 32, 32, 384)
        DI = int(0.5 * DM)
        N = 16
        R = -(-DM // 16)
        K = 4

        def selective_scan(xs, dts, As, Bs, Cs, Dsk):
            u = jnp.moveaxis(xs, -1, 0)
            d = jnp.moveaxis(dts, -1, 0)
            Bt = jnp.moveaxis(Bs, -1, 0)
            Ct = jnp.moveaxis(Cs, -1, 0)

            def step(h, inp):
                u_t, d_t, B_t, C_t = inp
                dA = jnp.exp(d_t[..., None] * As)
                h = h * dA + (d_t * u_t)[..., None] * B_t[:, :, None, :]
                y = jnp.einsum('bkcn,bkn->bkc', h, C_t)
                return (h, y)
            h0 = jnp.zeros(u.shape[1:] + (As.shape[-1],), u.dtype)
            _, ys = jax.lax.scan(step, h0, (u, d, Bt, Ct))
            ys = jnp.moveaxis(ys, 0, -1)
            return ys + Dsk[None, :, :, None] * xs
        key = jax.random.key(seed)
        ks = jax.random.split(key, 8)
        s = lambda i, shape, sc=0.02: jax.random.normal(ks[i], shape, jnp.float32) * sc
        return dict(x=jax.random.normal(ks[0], (B_, H_, W_, DM), jnp.float32), in_proj_w=s(1, (2 * DI, DM)), conv_w=s(2, (DI, 1, 3, 3)), conv_b=jnp.zeros((DI,), jnp.float32), x_proj_w=s(3, (K, R + 2 * N, DI)), dt_projs_w=s(4, (K, DI, R)), dt_projs_b=s(5, (K, DI)), A_logs=jnp.log(jnp.tile(jnp.arange(1, N + 1, dtype=jnp.float32)[None, :], (K * DI, 1))), Ds=jnp.ones((K * DI,), jnp.float32), out_norm_g=jnp.ones((DI,), jnp.float32), out_norm_b=jnp.zeros((DI,), jnp.float32), out_proj_w=s(6, (DM, DI)))
    _L0_conv_all = _L0_conv_setup()
    _L0_conv_in = {k: v for k, v in _L0_conv_all.items() if k in ('in_proj_w', 'conv_w', 'conv_b', 'x_proj_w', 'dt_projs_w', 'dt_projs_b', 'A_logs', 'Ds', 'out_norm_g', 'out_norm_b', 'out_proj_w')}
    del _L0_conv_all

    def _L1_conv_setup():
        import jax, jax.numpy as jnp
        import numpy as np
        DIM = 384
        NUM_HEADS = 12
        HEAD_DIM = DIM // NUM_HEADS
        HH = 48
        WW = 48
        REL_LEN = 2 * HH - 1
        THETA = 10000.0

        def _rope_freqs(dim, end_x, end_y, theta=THETA):
            freqs = 1.0 / theta ** (jnp.arange(0, dim, 4)[:dim // 4].astype(jnp.float32) / dim)
            t = jnp.arange(end_x * end_y, dtype=jnp.float32)
            t_x = t % end_x
            t_y = jnp.floor(t / end_x)
            f = jnp.concatenate([t_x[:, None] * freqs[None, :], t_y[:, None] * freqs[None, :]], axis=-1)
            return (jnp.cos(f), jnp.sin(f))

        def _rel_bias(size, rel_pos):
            coords = jnp.arange(size)[:, None] - jnp.arange(size)[None, :] + (size - 1)
            return rel_pos[coords]
        key = jax.random.key(seed)
        ks = jax.random.split(key, 6)
        x = jax.random.normal(ks[0], (1, HH, WW, DIM), dtype=jnp.float32)
        w_qkv = jax.random.normal(ks[1], (DIM, 3 * DIM), dtype=jnp.float32) * 0.02
        b_qkv = jnp.zeros((3 * DIM,), dtype=jnp.float32)
        w_proj = jax.random.normal(ks[2], (DIM, DIM), dtype=jnp.float32) * 0.02
        b_proj = jnp.zeros((DIM,), dtype=jnp.float32)
        rel_pos_h = jax.random.normal(ks[3], (REL_LEN, HEAD_DIM), dtype=jnp.float32) * 0.02
        rel_pos_w = jax.random.normal(ks[4], (REL_LEN, HEAD_DIM), dtype=jnp.float32) * 0.02
        return {'x': x, 'w_qkv': w_qkv, 'b_qkv': b_qkv, 'w_proj': w_proj, 'b_proj': b_proj, 'rel_pos_h': rel_pos_h, 'rel_pos_w': rel_pos_w}
    _L1_conv_all = _L1_conv_setup()
    _L1_conv_in = {k: v for k, v in _L1_conv_all.items() if k in ('w_qkv', 'b_qkv', 'w_proj', 'b_proj', 'rel_pos_h', 'rel_pos_w')}
    del _L1_conv_all
    return {'x': x, 'L0_conv_in_proj_w': _L0_conv_in['in_proj_w'], 'L0_conv_conv_w': _L0_conv_in['conv_w'], 'L0_conv_conv_b': _L0_conv_in['conv_b'], 'L0_conv_x_proj_w': _L0_conv_in['x_proj_w'], 'L0_conv_dt_projs_w': _L0_conv_in['dt_projs_w'], 'L0_conv_dt_projs_b': _L0_conv_in['dt_projs_b'], 'L0_conv_A_logs': _L0_conv_in['A_logs'], 'L0_conv_Ds': _L0_conv_in['Ds'], 'L0_conv_out_norm_g': _L0_conv_in['out_norm_g'], 'L0_conv_out_norm_b': _L0_conv_in['out_norm_b'], 'L0_conv_out_proj_w': _L0_conv_in['out_proj_w'], 'L1_conv_w_qkv': _L1_conv_in['w_qkv'], 'L1_conv_b_qkv': _L1_conv_in['b_qkv'], 'L1_conv_w_proj': _L1_conv_in['w_proj'], 'L1_conv_b_proj': _L1_conv_in['b_proj'], 'L1_conv_rel_pos_h': _L1_conv_in['rel_pos_h'], 'L1_conv_rel_pos_w': _L1_conv_in['rel_pos_w']}

def reference(x, L0_conv_in_proj_w, L0_conv_conv_w, L0_conv_conv_b, L0_conv_x_proj_w, L0_conv_dt_projs_w, L0_conv_dt_projs_b, L0_conv_A_logs, L0_conv_Ds, L0_conv_out_norm_g, L0_conv_out_norm_b, L0_conv_out_proj_w, L1_conv_w_qkv, L1_conv_b_qkv, L1_conv_w_proj, L1_conv_b_proj, L1_conv_rel_pos_h, L1_conv_rel_pos_w):
    import jax
    import jax.numpy as jnp

    def _L0_conv_ref(x, in_proj_w, conv_w, conv_b, x_proj_w, dt_projs_w, dt_projs_b, A_logs, Ds, out_norm_g, out_norm_b, out_proj_w):
        import jax, jax.numpy as jnp
        import numpy as np
        B_, H_, W_, DM = (4, 32, 32, 384)
        DI = int(0.5 * DM)
        N = 16
        R = -(-DM // 16)
        K = 4

        def selective_scan(xs, dts, As, Bs, Cs, Dsk):
            u = jnp.moveaxis(xs, -1, 0)
            d = jnp.moveaxis(dts, -1, 0)
            Bt = jnp.moveaxis(Bs, -1, 0)
            Ct = jnp.moveaxis(Cs, -1, 0)

            def step(h, inp):
                u_t, d_t, B_t, C_t = inp
                dA = jnp.exp(d_t[..., None] * As)
                h = h * dA + (d_t * u_t)[..., None] * B_t[:, :, None, :]
                y = jnp.einsum('bkcn,bkn->bkc', h, C_t)
                return (h, y)
            h0 = jnp.zeros(u.shape[1:] + (As.shape[-1],), u.dtype)
            _, ys = jax.lax.scan(step, h0, (u, d, Bt, Ct))
            ys = jnp.moveaxis(ys, 0, -1)
            return ys + Dsk[None, :, :, None] * xs
        B, H, W, _ = x.shape
        L = H * W
        xz = x @ in_proj_w.T
        xh, z = jnp.split(xz, 2, axis=-1)
        xc = jnp.transpose(xh, (0, 3, 1, 2))
        xc = jax.lax.conv_general_dilated(xc, conv_w, (1, 1), 'SAME', feature_group_count=DI)
        xc = jax.nn.silu(xc + conv_b[None, :, None, None])
        x_flat = xc.reshape(B, DI, L)
        x_t = jnp.transpose(xc, (0, 1, 3, 2)).reshape(B, DI, L)
        x_hwwh = jnp.stack([x_flat, x_t], 1)
        xs = jnp.concatenate([x_hwwh, jnp.flip(x_hwwh, -1)], 1)
        x_dbl = jnp.einsum('bkdl,kcd->bkcl', xs, x_proj_w)
        dts, Bs, Cs = jnp.split(x_dbl, [R, R + N], axis=2)
        dts = jnp.einsum('bkrl,kdr->bkdl', dts, dt_projs_w)
        dts = jax.nn.softplus(dts + dt_projs_b[None, :, :, None])
        As = -jnp.exp(A_logs).reshape(K, DI, N)
        out_y = selective_scan(xs, dts, As, Bs, Cs, Ds.reshape(K, DI))
        inv_y = jnp.flip(out_y[:, 2:4], -1)
        wh_y = jnp.transpose(out_y[:, 1].reshape(B, DI, W, H), (0, 1, 3, 2)).reshape(B, DI, L)
        invwh_y = jnp.transpose(inv_y[:, 1].reshape(B, DI, W, H), (0, 1, 3, 2)).reshape(B, DI, L)
        y = out_y[:, 0] + inv_y[:, 0] + wh_y + invwh_y
        y = jnp.transpose(y, (0, 2, 1)).reshape(B, H, W, DI)
        mu = y.mean(-1, keepdims=True)
        var = y.var(-1, keepdims=True)
        y = (y - mu) / jnp.sqrt(var + 1e-05) * out_norm_g + out_norm_b
        y = y * jax.nn.silu(z)
        return y @ out_proj_w.T

    def _L1_conv_ref(x, w_qkv, b_qkv, w_proj, b_proj, rel_pos_h, rel_pos_w):
        import jax, jax.numpy as jnp
        import numpy as np
        DIM = 384
        NUM_HEADS = 12
        HEAD_DIM = DIM // NUM_HEADS
        HH = 48
        WW = 48
        REL_LEN = 2 * HH - 1
        THETA = 10000.0

        def _rope_freqs(dim, end_x, end_y, theta=THETA):
            freqs = 1.0 / theta ** (jnp.arange(0, dim, 4)[:dim // 4].astype(jnp.float32) / dim)
            t = jnp.arange(end_x * end_y, dtype=jnp.float32)
            t_x = t % end_x
            t_y = jnp.floor(t / end_x)
            f = jnp.concatenate([t_x[:, None] * freqs[None, :], t_y[:, None] * freqs[None, :]], axis=-1)
            return (jnp.cos(f), jnp.sin(f))

        def _rel_bias(size, rel_pos):
            coords = jnp.arange(size)[:, None] - jnp.arange(size)[None, :] + (size - 1)
            return rel_pos[coords]
        B, H, W, dim = x.shape
        L = H * W
        nh, hd = (NUM_HEADS, dim // NUM_HEADS)
        scale = hd ** (-0.5)
        qkv = (x.reshape(B, L, dim) @ w_qkv + b_qkv).reshape(B, L, 3, nh, hd)
        qkv = qkv.transpose(2, 0, 3, 1, 4)
        q, k, v = (qkv[0], qkv[1], qkv[2])
        cosf, sinf = _rope_freqs(hd, W, H)
        c = cosf[None, None]
        s = sinf[None, None]

        def rot(t):
            tr = t.reshape(B, nh, L, hd // 2, 2)
            t0, t1 = (tr[..., 0], tr[..., 1])
            return jnp.stack([t0 * c - t1 * s, t0 * s + t1 * c], axis=-1).reshape(B, nh, L, hd)
        q = rot(q)
        k = rot(k)
        attn = jnp.einsum('bnqd,bnkd->bnqk', q, k) * scale
        bias_h = _rel_bias(H, rel_pos_h)
        bias_w = _rel_bias(W, rel_pos_w)
        q6 = q.reshape(B, nh, H, W, hd)
        rel_h = jnp.einsum('bnhwc,hkc->bnhwk', q6, bias_h)
        rel_w = jnp.einsum('bnhwc,wkc->bnhwk', q6, bias_w)
        attn = attn.reshape(B, nh, H, W, H, W) + rel_h[..., :, None] + rel_w[..., None, :]
        attn = attn.reshape(B, nh, L, L)
        attn = jax.nn.softmax(attn, axis=-1)
        out = jnp.einsum('bnqk,bnkd->bnqd', attn, v)
        out = out.transpose(0, 2, 1, 3).reshape(B, H, W, dim)
        return out @ w_proj + b_proj

    def _gn(v, G=32, eps=1e-05):
        B_, H_, W_, C_ = v.shape
        g = v.reshape(B_, H_, W_, G, C_ // G)
        m = jnp.mean(g, axis=(1, 2, 4), keepdims=True)
        s = jnp.var(g, axis=(1, 2, 4), keepdims=True)
        return ((g - m) / jnp.sqrt(s + eps)).reshape(v.shape)

    def _ln_c(v, eps=1e-06):
        m = jnp.mean(v, axis=-1, keepdims=True)
        s = jnp.var(v, axis=-1, keepdims=True)
        return (v - m) / jnp.sqrt(s + eps)

    def _ln_t(v, eps=1e-05):
        m = jnp.mean(v, axis=-1, keepdims=True)
        s = jnp.var(v, axis=-1, keepdims=True)
        return (v - m) / jnp.sqrt(s + eps)

    def _to_tokens(v):
        B_, H_, W_, C_ = v.shape
        return v.reshape(B_, H_ * W_, C_)

    def _from_tokens(t, like):
        return t.reshape(like.shape)
    x = x + _L0_conv_ref(_gn(x), L0_conv_in_proj_w, L0_conv_conv_w, L0_conv_conv_b, L0_conv_x_proj_w, L0_conv_dt_projs_w, L0_conv_dt_projs_b, L0_conv_A_logs, L0_conv_Ds, L0_conv_out_norm_g, L0_conv_out_norm_b, L0_conv_out_proj_w)
    x = x + _L1_conv_ref(_gn(x), L1_conv_w_qkv, L1_conv_b_qkv, L1_conv_w_proj, L1_conv_b_proj, L1_conv_rel_pos_h, L1_conv_rel_pos_w)
    return x

_drawn_inputs = setup_inputs


def setup_inputs(seed=0):
    import zlib

    import numpy as np

    out = dict(_drawn_inputs(seed))
    spreads = {'L0_conv_conv_b': (0.0, 0.1),
     'L0_conv_Ds': (1.0, 0.6),
     'L0_conv_out_norm_g': (1.0, 0.6),
     'L0_conv_out_norm_b': (0.0, 0.8),
     'L1_conv_b_qkv': (0.0, 0.1),
     'L1_conv_b_proj': (0.0, 0.1)}
    factors = {'L0_conv_conv_w': 3.76,
     'L0_conv_x_proj_w': 64.0,
     'L0_conv_dt_projs_w': 64.0,
     'L0_conv_dt_projs_b': 64.0,
     'L0_conv_A_logs': 64.0,
     'L1_conv_w_qkv': 8.0,
     'L1_conv_rel_pos_h': 8.0,
     'L1_conv_rel_pos_w': 8.0}
    for name, (base, spread) in spreads.items():
        noise = np.random.default_rng([zlib.crc32(name.encode()), seed]).standard_normal(out[name].shape)
        drawn = base * np.exp(spread * noise) if base else spread * noise
        out[name] = jnp.asarray(drawn.astype(out[name].dtype))
    for name, factor in factors.items():
        out[name] = (out[name] * factor).astype(out[name].dtype)
    return out
```

```python
from contextlib import ExitStack

import concourse.bass as bass
from concourse import mybir

P = 128
B, IMG, C = 4, 32, 384
L = IMG * IMG
CT = C // P
HALF = L // 2
DI, NST, RANK, DIRS = 192, 16, 24, 4
SEQ = DIRS * DI // P
XT = 64
ITEMS = SEQ * NST
NH, HD = 12, 32
HG = P // HD
GROUPS = NH // HG
QB = L // P
STEPS = QB * HG
REL = 2 * IMG - 1
ATT_SCALE = float(HD) ** -0.5
GN_EPS = 1e-5
LN_EPS = 1e-5
SMALL = 2.0 ** -7
A_LOG_MAX = 80.0
TILE_ORDER = [0, 3, 1, 4, 2, 5]

F32 = mybir.dt.float32
BF16 = mybir.dt.bfloat16
U8 = mybir.dt.uint8
ALU = mybir.AluOpType
ACT = mybir.ActivationFunctionType
AX_X = mybir.AxisListType.X

MATS = {
    "w_in": (3 * P, C), "w_xdbl": (3 * P, 2 * P), "w_dt": (P, SEQ * P), "w_out": (2 * P, C),
    "w_qkv": (3 * P, 3 * C), "w_proj": (3 * P, C), "group_mean": (3 * P, C),
    "cos": (P, L), "sin": (P, L), "ident": (P, P), "to_low": (P, P), "to_high": (P, P), "turn": (P, P),
    "chan_mean": (P, P), "head_rows": (NH, C), "rel_h": (HD, REL), "rel_w": (HD, REL),
}
COLS = {
    "conv_w": 2 * 9, "conv_b": 2, "dt_b": SEQ, "a_log": SEQ * NST, "skip": 2 * DIRS,
    "norm_g": 2, "norm_b": 2, "b_qkv": 9, "b_proj": 3,
}


class Signal:

    def __init__(self, sem, per_image, unit=1):
        self.sem, self.per_image, self.unit = sem, per_image, unit

    def after(self, b, n):
        return n * self.unit


def build(nc, x, mats, cols, sel_in, onehot, out):
    ctx = ExitStack()
    with ctx:
        def sb(name, shape, dt=F32):
            return ctx.enter_context(nc.sbuf_tensor(name, shape, dt))

        def signal(name, per_image, unit=1):
            return Signal(ctx.enter_context(nc.semaphore(name)), per_image, unit)

        X = sb("residual", [P, CT, L])
        XN = sb("normed", [P, CT, L])
        W = {}
        for name, (rows, width) in MATS.items():
            W[name] = sb(name, [min(rows, P), max(rows // P, 1), width])
        COL = {name: sb(name, [P, width]) for name, width in COLS.items()}
        SEL = sb("selectors", [3 * 2 * NST, 3 * NST, P], BF16)
        one = sb("one", [P, 1])
        a_neg = sb("a_neg", [P, SEQ * NST])
        a_low = sb("a_low", [P, SEQ * NST])
        a_inf = sb("a_inf", [P, SEQ * NST])
        skip_sum = sb("skip_sum", [P, 2])
        bk_scaled = sb("bk_scaled", [P, GROUPS])
        bn = sb("bn", [P, CT, 2, 6])
        mv = sb("mv", [P, CT, 2])
        gs = sb("gs", [P, CT, 2])
        g_tmp = sb("g_tmp", [P, CT])
        g_rstd = sb("g_rstd", [P, CT])
        neg_max = sb("neg_max", [P, 4])
        row_sum = sb("row_sum", [P, QB, NH])
        arena = sb("arena", [P, 30 * L])
        PS = ctx.enter_context(nc.psum_tensor("PS", [P, 8 * HALF], F32))

        def unit(k, n=1):
            return arena[:, k * L:(k + n) * L]

        def units(k, n):
            return unit(k, n).rearrange("p (n l) -> p n l", n=n)

        def banks(k, n=2):
            return PS[:, k * HALF:(k + n) * HALF]

        U, YSB, ZS, DTS = units(0, 3), units(3, 3), units(6, 2), unit(8)
        BCS = unit(9, 2).bitcast(BF16).rearrange("p (g l) -> p g l", g=4)
        DELTA, DU = units(11, 2), units(13, 2)
        SE, SQ3, SR = unit(15), unit(16), unit(17)
        MASK = unit(18)[:, 0:L // 4].bitcast(U8)
        DA, BSB, DBU, HS, HC = units(19, 3), units(22, 2), units(24, 2), units(26, 2), units(28, 2)
        CONV = units(19, 2)
        BCP = arena[:, 21 * L:22 * L + HALF].bitcast(BF16).rearrange("p (a l) -> p a l", a=3)
        REST = units(23, 2)
        YF, SQ, RSTD = units(19, 2), units(21, 2), unit(23)
        QX = units(0, 4)
        KX = units(4, 4)
        V = unit(8, 3).rearrange("p (t c) -> p t c", t=QB)
        PR = units(11, 2)
        PT = unit(13, 8).rearrange("p (s j t q) -> p s j t q", s=2, j=HG, t=QB)
        QKB = units(21, 2)
        RT1, RT2 = unit(23), unit(27)
        OT = units(24, 3)
        RT = unit(28)
        OUT = units(13, 3)

        consts = signal("consts_loaded", 0, 16)
        prep = signal("consts_prepared", 0)
        a_exp = ctx.enter_context(nc.semaphore("a_exp"))
        image_done = ctx.enter_context(nc.semaphore("image_done"))
        clearing = ctx.enter_context(nc.semaphore("clearing"))
        image_open = ctx.enter_context(nc.semaphore("image_open"))
        x_loaded = signal("x_loaded", 1, 16)
        gn_stats = signal("gn_stats", 2)
        gn_psum = signal("gn_psum", 2)
        gn_var = signal("gn_var", 2)
        gn_rstd = signal("gn_rstd", 2)
        xn_ready = signal("xn_ready", 2)
        xh_psum = signal("xh_psum", 2)
        z_psum = signal("z_psum", 1)
        conv_done = signal("conv_done", 2)
        u_ready = signal("u_ready", 1)
        xdbl_psum = signal("xdbl_psum", 1)
        dts_saved = signal("dts_saved", 1)
        bc_hi = signal("bc_hi", 1)
        bc_split = signal("bc_split", 1)
        bcs_loaded = signal("bcs_loaded", 12, 16)
        bslot_full = signal("bslot_full", ITEMS + SEQ)
        bslot_free = signal("bslot_free", ITEMS + SEQ)
        cslot_full = signal("cslot_full", ITEMS)
        soft_e = signal("soft_e", SEQ)
        soft_ln = signal("soft_ln", SEQ)
        soft_q = signal("soft_q", SEQ)
        soft_q3 = signal("soft_q3", SEQ)
        soft_log = signal("soft_log", SEQ)
        delta_ready = signal("delta_ready", SEQ)
        du_ready = signal("du_ready", SEQ)
        da_ready = signal("da_ready", ITEMS)
        bsb_ready = signal("bsb_ready", ITEMS)
        dbu_ready = signal("dbu_ready", ITEMS)
        scan_done = signal("scan_done", ITEMS)
        hc_ready = signal("hc_ready", ITEMS)
        acc_done = signal("acc_done", ITEMS)
        y_saved = signal("y_saved", 3)
        y_psum = signal("y_psum", 1)
        yf_ready = signal("yf_ready", 1)
        mean_psum = signal("mean_psum", 1)
        yc_ready = signal("yc_ready", 1)
        sq_ready = signal("sq_ready", 1)
        var_psum = signal("var_psum", 1)
        rstd_ready = signal("rstd_ready", 1)
        yg_ready = signal("yg_ready", 1)
        op_psum = signal("op_psum", 1)
        v_psum = signal("v_psum", QB)
        v_saved = signal("v_saved", QB)
        onehot_loaded = signal("onehot_loaded", HG, 16)
        qk_psum = signal("qk_psum", 2 * GROUPS)
        qk_saved = signal("qk_saved", 2 * GROUPS)
        turn_psum = signal("turn_psum", 2 * GROUPS)
        rope_ready = signal("rope_ready", 2 * GROUPS)
        q_loaded = signal("q_loaded", HG * GROUPS, 16)
        k_loaded = signal("k_loaded", HG * GROUPS, 16)
        rel_psum = signal("rel_psum", 4 * GROUPS)
        relh_saved = signal("relh_saved", 4 * GROUPS)
        relw_saved = signal("relw_saved", 4 * GROUPS)
        s_psum = signal("s_psum", STEPS * GROUPS)
        max_done = signal("max_done", STEPS * GROUPS)
        exp_done = signal("exp_done", STEPS * GROUPS)
        pt_psum = signal("pt_psum", STEPS * GROUPS)
        pt_saved = signal("pt_saved", STEPS * GROUPS)
        o_psum = signal("o_psum", QB * GROUPS)
        o_saved = signal("o_saved", QB * GROUPS)
        rs_ready = signal("rs_ready", 1)
        rt_psum = signal("rt_psum", 1)
        rt_saved = signal("rt_saved", 1)
        rb_psum = signal("rb_psum", 1)
        on_ready = signal("on_ready", 1)
        pj_psum = signal("pj_psum", 1)
        out_ready = signal("out_ready", 1)
        out_stored = signal("out_stored", 1, 16)
        dve_step = signal("dve_step", 0)
        act_step = signal("act_step", 0)

        def steps(eng, sig, b):
            count = [0]

            def link(ins):
                count[0] += 1
                ins.then_inc(sig.sem, 1)
                eng.wait_ge(sig.sem, sig.after(b, count[0]))
            return link

        first, last_sem = x_loaded.sem, act_step.sem
        per_image = range(first.num, last_sem.num + 1)

        def leave_image(eng, b):
            eng.sem_inc(image_done, 1)
            eng.wait_ge(image_open, b + 1)

        N_CONST = len(MATS) + len(COLS) + 1
        block = ctx.enter_context(nc.Block())

        @block.sync
        def _(sp):
            for name, (rows, width) in MATS.items():
                k = max(rows // P, 1)
                sp.dma_start(W[name][:, :, :], mats[name].rearrange("(k p) c -> p k c", k=k)).then_inc(consts.sem, 16)
            for name in COLS:
                sp.dma_start(COL[name][:, :], cols[name]).then_inc(consts.sem, 16)
            sp.dma_start(SEL[:, :, :], sel_in).then_inc(consts.sem, 16)
            with sp.Fori(0, B) as b:
                sp.dma_start(X[:, :, :], x[bass.ds(b, 1), :, :].rearrange("o (k p) l -> p (o k) l", p=P)
                             ).then_inc(x_loaded.sem, 16)
                sp.wait_ge(bc_split.sem, bc_split.after(b, 1))
                for part in range(3):
                    for g in range(4):
                        sp.dma_start(BCS[32 * part:32 * part + 32, g, :], BCP[32 * g:32 * g + 32, part, :]
                                     ).then_inc(bcs_loaded.sem, 16)
                sp.wait_ge(xn_ready.sem, xn_ready.after(b, 2))
                for j in range(HG):
                    sp.dma_start(KX[HD:3 * HD, j, :], onehot).then_inc(onehot_loaded.sem, 16)
                for g in range(GROUPS):
                    for side, dst, loaded in ((0, QX, q_loaded), (1, KX, k_loaded)):
                        sp.wait_ge(rope_ready.sem, rope_ready.after(b, 2 * g + side + 1))
                        if g:
                            sp.wait_ge(s_psum.sem, s_psum.after(b, STEPS * g))
                        for j in range(HG):
                            sp.dma_start(dst[0:HD, j, :], QKB[HD * j:HD * j + HD, side, :]
                                         ).then_inc(loaded.sem, 16)
                sp.wait_ge(out_ready.sem, out_ready.after(b, 1))
                sp.dma_start(out[bass.ds(b, 1), :, :].rearrange("o (k p) l -> p (o k) l", p=P), OUT[:, :, :]
                             ).then_inc(out_stored.sem, 16)
                sp.wait_ge(out_stored.sem, out_stored.after(b, 1))
                sp.wait_ge(image_done, 4 * b + 4)
                sp.sem_inc(clearing, 1)
                sp.sem_clear(per_image)
                sp.sem_inc(image_open, 1)

        @block.tensor
        def _(pe):
            pe.wait_ge(consts.sem, 16 * N_CONST)
            pe.wait_ge(prep.sem, 4)

            def product(dst, pairs):
                for h in range(2):
                    for k, (lhs, rhs) in enumerate(pairs):
                        last = pe.matmul(dst[:, h * HALF:(h + 1) * HALF], lhs, rhs(h),
                                         start=(k == 0), stop=(k == len(pairs) - 1))
                return last

            def flat(ap):
                return lambda h: ap[:, h * HALF:(h + 1) * HALF]

            def turned(ap):
                return lambda h: ap.rearrange("p (w h) -> p h w", h=IMG)[:, h * (IMG // 2):(h + 1) * (IMG // 2), :]

            def group_stats(b, n):
                pe.wait_ge(gn_stats.sem, gn_stats.after(b, n))
                for m in range(CT):
                    for k in range(CT):
                        last = pe.matmul(PS[:, 6 * HALF + 2 * m:6 * HALF + 2 * m + 2],
                                         W["group_mean"][:, k, m * P:(m + 1) * P], mv[:, k, :],
                                         start=(k == 0), stop=(k == CT - 1), skip_group_check=True)
                last.then_inc(gn_psum.sem, 1)

            with pe.Fori(0, B) as b:
                group_stats(b, 1)
                pe.wait_ge(xn_ready.sem, xn_ready.after(b, 1))
                xn = [flat(XN[:, k, :]) for k in range(CT)]
                for m, (c0, rows, bank) in enumerate([(0, P, 0), (P, XT, 2), (DI, P, 4), (DI + P, XT, 6)]):
                    last = product(banks(bank)[0:rows, :],
                                   [(W["w_in"][:, k, c0:c0 + rows], xn[k]) for k in range(CT)])
                    if m < 2:
                        last.then_inc(xh_psum.sem, 1)
                last.then_inc(z_psum.sem, 1)
                pe.wait_ge(u_ready.sem, u_ready.after(b, 1))
                us = [flat(U[:, k, :]) for k in range(3)]
                product(banks(0), [(W["w_xdbl"][:, k, 0:P], us[k]) for k in range(3)])
                product(banks(2), [(W["w_xdbl"][:, k, P:2 * P], us[k]) for k in range(3)]
                        ).then_inc(xdbl_psum.sem, 1)

                slot = [0]

                def b_slot():
                    if slot[0]:
                        pe.wait_ge(bslot_free.sem, bslot_free.after(b, slot[0]))
                    slot[0] += 1

                def dt_product(s):
                    b_slot()
                    t = TILE_ORDER[s]
                    product(banks(0), [(W["w_dt"][:, 0, t * P:(t + 1) * P], flat(DTS))]
                            ).then_inc(bslot_full.sem, 1)

                def broadcast(dst, i, c):
                    s, n = divmod(i, NST)
                    t = TILE_ORDER[s]
                    return product(dst, [(SEL[:, (t % 3) * NST + n, :], flat(BCS[0:96, 2 * (t // 3) + c, :]))])

                def accumulate(i):
                    pe.wait_ge(hc_ready.sem, hc_ready.after(b, i + 1))
                    pair, k = divmod(i, 2 * NST)
                    if k == 0 and pair:
                        pe.wait_ge(y_saved.sem, y_saved.after(b, pair))
                    for h in range(2):
                        last = pe.matmul(banks(6)[:, h * HALF:(h + 1) * HALF], W["ident"][:, 0, :],
                                         HC[:, i % 2, h * HALF:(h + 1) * HALF],
                                         start=(k == 0), stop=(k == 2 * NST - 1), skip_group_check=True)
                    last.then_inc(acc_done.sem, 1)

                pe.wait_ge(dts_saved.sem, dts_saved.after(b, 1))
                pe.wait_ge(bc_split.sem, bc_split.after(b, 1))
                dt_product(0)
                pe.wait_ge(bcs_loaded.sem, bcs_loaded.after(b, 12))
                for i in range(ITEMS):
                    s, n = divmod(i, NST)
                    b_slot()
                    broadcast(banks(0), i, 0).then_inc(bslot_full.sem, 1)
                    if i >= 2:
                        pe.wait_ge(hc_ready.sem, hc_ready.after(b, i - 1))
                    broadcast(banks(2 + 2 * (i % 2)), i, 1).then_inc(cslot_full.sem, 1)
                    if n == NST // 2 and s < SEQ - 1:
                        dt_product(s + 1)
                    if i >= 2:
                        accumulate(i - 2)
                accumulate(ITEMS - 2)
                accumulate(ITEMS - 1)

                pe.wait_ge(y_saved.sem, y_saved.after(b, 3))
                low, high, idn = W["to_low"][:, 0, :], W["to_high"][:, 0, :], W["ident"][:, 0, :]
                product(banks(0), [(idn, flat(YSB[:, 0, :])), (low, turned(YSB[:, 1, :])),
                                   (high, turned(YSB[:, 2, :]))])
                product(banks(2)[0:XT, :], [(idn[:, 0:XT], flat(YSB[:, 1, :])),
                                            (low[:, 0:XT], turned(YSB[:, 2, :]))]
                        ).then_inc(y_psum.sem, 1)
                cm = W["chan_mean"][:, 0, :]
                pe.wait_ge(yf_ready.sem, yf_ready.after(b, 1))
                product(banks(4), [(cm, flat(YF[:, 0, :])), (cm[0:XT, :], flat(YF[0:XT, 1, :]))]
                        ).then_inc(mean_psum.sem, 1)
                pe.wait_ge(sq_ready.sem, sq_ready.after(b, 1))
                product(banks(6), [(cm, flat(SQ[:, 0, :])), (cm[0:XT, :], flat(SQ[0:XT, 1, :]))]
                        ).then_inc(var_psum.sem, 1)
                pe.wait_ge(yg_ready.sem, yg_ready.after(b, 1))
                for m in range(CT):
                    last = product(banks(2 * m), [(W["w_out"][:, 0, m * P:(m + 1) * P], flat(YF[:, 0, :])),
                                                  (W["w_out"][0:XT, 1, m * P:(m + 1) * P], flat(YF[0:XT, 1, :]))])
                last.then_inc(op_psum.sem, 1)

                group_stats(b, 2)
                pe.wait_ge(xn_ready.sem, xn_ready.after(b, 2))
                for t in range(QB):
                    for k in range(CT):
                        last = pe.matmul(banks(t, 1)[:, 0:C], XN[:, k, t * P:(t + 1) * P],
                                         W["w_qkv"][:, k, 2 * C:3 * C], start=(k == 0), stop=(k == CT - 1))
                    last.then_inc(v_psum.sem, 1)
                for g in range(GROUPS):
                    for side in range(2):
                        if g == 0:
                            pe.wait_ge(v_saved.sem, v_saved.after(b, QB))
                        elif side == 0:
                            pe.wait_ge(exp_done.sem, exp_done.after(b, STEPS * g))
                        product(banks(2 * side), [(W["w_qkv"][:, k, side * C + g * P:side * C + (g + 1) * P], xn[k])
                                                  for k in range(CT)]).then_inc(qk_psum.sem, 1)
                    for side in range(2):
                        pe.wait_ge(qk_saved.sem, qk_saved.after(b, 2 * g + side + 1))
                        if g and side == 0:
                            pe.wait_ge(pt_saved.sem, pt_saved.after(b, STEPS * g))
                            pe.wait_ge(o_saved.sem, o_saved.after(b, QB * g))
                        product(banks(4 + 2 * side), [(W["turn"][:, 0, :], flat(QKB[:, side, :]))]
                                ).then_inc(turn_psum.sem, 1)
                    pe.wait_ge(q_loaded.sem, q_loaded.after(b, HG * (g + 1)))
                    qv = QX.rearrange("p j (h w) -> p j h w", h=IMG)
                    for c in range(4):
                        if c >= 2:
                            pe.wait_ge(relh_saved.sem, relh_saved.after(b, 4 * g + c - 1))
                            pe.wait_ge(relw_saved.sem, relw_saved.after(b, 4 * g + c - 1))
                        for r in range(8):
                            at = 8 * c + r
                            dst = banks(2 * (c % 2))[:, r * P:(r + 1) * P]
                            pe.matmul(dst[HD:2 * HD, :], W["rel_h"][0:HD, 0, IMG - 1 - at:REL - at],
                                      qv[0:HD, :, at, :], start=True, stop=True, skip_group_check=True)
                            last = pe.matmul(dst[2 * HD:3 * HD, :], W["rel_w"][0:HD, 0, IMG - 1 - at:REL - at],
                                             qv[0:HD, :, :, at], start=True, stop=True, skip_group_check=True)
                        last.then_inc(rel_psum.sem, 1)

                    def scores(k):
                        s = STEPS * g + k
                        qb, j = divmod(k, HG)
                        if k >= 2:
                            pe.wait_ge(exp_done.sem, exp_done.after(b, s - 1))
                        product(banks(2 * (k % 2)), [(QX[0:3 * HD, j, qb * P:(qb + 1) * P], flat(KX[0:3 * HD, j, :]))]
                                ).then_inc(s_psum.sem, 1)

                    def turn_probs(k):
                        s = STEPS * g + k
                        pe.wait_ge(exp_done.sem, exp_done.after(b, s + 1))
                        if s:
                            pe.wait_ge(pt_saved.sem, pt_saved.after(b, s))
                        for t in range(QB):
                            last = pe.transpose(banks(4)[:, t * P:(t + 1) * P],
                                                PR[:, k % 2, t * P:(t + 1) * P], idn)
                        last.then_inc(pt_psum.sem, 1)

                    def weigh(qb):
                        n = QB * g + qb
                        pe.wait_ge(pt_saved.sem, pt_saved.after(b, STEPS * g + HG * (qb + 1)))
                        if n >= 2:
                            pe.wait_ge(o_saved.sem, o_saved.after(b, n - 1))
                        for t in range(QB):
                            for j in range(HG):
                                head = HG * g + j
                                last = pe.matmul(banks(6 + qb % 2, 1)[HD * j:HD * j + HD, 0:P],
                                                 V[:, t, head * HD:(head + 1) * HD], PT[:, qb % 2, j, t, :],
                                                 start=(t == 0), stop=(t == QB - 1), skip_group_check=True)
                        last.then_inc(o_psum.sem, 1)

                    pe.wait_ge(relh_saved.sem, relh_saved.after(b, 4 * g + 4))
                    pe.wait_ge(relw_saved.sem, relw_saved.after(b, 4 * g + 4))
                    pe.wait_ge(k_loaded.sem, k_loaded.after(b, HG * (g + 1)))
                    if g == 0:
                        pe.wait_ge(onehot_loaded.sem, onehot_loaded.after(b, HG))
                    scores(0)
                    for k in range(STEPS):
                        if k + 1 < STEPS:
                            scores(k + 1)
                        if k % HG == 1 and k > HG:
                            weigh(k // HG - 1)
                        turn_probs(k)
                    weigh(QB - 1)

                pe.wait_ge(rs_ready.sem, rs_ready.after(b, 1))
                for t in range(QB):
                    last = pe.transpose(banks(0)[0:NH, t * P:(t + 1) * P], row_sum[:, t, :], idn)
                last.then_inc(rt_psum.sem, 1)
                pe.wait_ge(rt_saved.sem, rt_saved.after(b, 1))
                for g in range(GROUPS):
                    last = product(banks(2 + 2 * g), [(W["head_rows"][0:NH, 0, g * P:(g + 1) * P], flat(RT[0:NH, :]))])
                last.then_inc(rb_psum.sem, 1)
                pe.wait_ge(on_ready.sem, on_ready.after(b, 1))
                for m in range(CT):
                    last = product(banks(2 * m), [(W["w_proj"][:, k, m * P:(m + 1) * P], flat(OT[:, k, :]))
                                                  for k in range(CT)])
                last.then_inc(pj_psum.sem, 1)
                leave_image(pe, b)

        @block.vector
        def _(dve):
            dve.memset(one[:, :], 1.0)
            dve.wait_ge(consts.sem, 16 * N_CONST)
            dve.tensor_scalar(a_inf[:, :], COL["a_log"][:, :], A_LOG_MAX, -200.0, ALU.is_gt, ALU.mult)
            dve.tensor_scalar(a_low[:, :], COL["a_log"][:, :], A_LOG_MAX, None, ALU.min).then_inc(prep.sem, 1)
            sk = COL["skip"][:, :].rearrange("p (m k) -> p m k", m=2)
            dve.tensor_reduce(skip_sum[:, :], sk, AX_X, ALU.add).then_inc(prep.sem, 1)
            dve.tensor_scalar(bk_scaled[:, :], COL["b_qkv"][:, 3:6], ATT_SCALE, None, ALU.mult).then_inc(prep.sem, 1)
            dve.wait_ge(prep.sem, 4)

            with dve.Fori(0, B) as b:
                link = steps(dve, dve_step, b)

                def group_norm(n):
                    for k in range(CT):
                        for h in range(2):
                            last = dve.bn_stats(bn[:, k, h, :], X[:, k, h * HALF:(h + 1) * HALF])
                    link(last)
                    for k in range(CT):
                        last = dve.bn_aggr(mv[:, k, :], bn[:, k, :, :])
                    link(last)
                    link(dve.tensor_tensor(g_tmp[:, :], mv[:, :, 0], mv[:, :, 0], ALU.mult))
                    dve.tensor_tensor(mv[:, :, 1], mv[:, :, 1], g_tmp[:, :], ALU.add).then_inc(gn_stats.sem, 1)
                    dve.wait_ge(gn_psum.sem, gn_psum.after(b, n))
                    link(dve.tensor_copy(gs[:, :, :], PS[:, 6 * HALF:6 * HALF + 2 * CT].rearrange("p (m t) -> p m t", t=2)))
                    link(dve.tensor_tensor(g_tmp[:, :], gs[:, :, 0], gs[:, :, 0], ALU.mult))
                    link(dve.tensor_tensor(g_tmp[:, :], gs[:, :, 1], g_tmp[:, :], ALU.subtract))
                    dve.tensor_scalar(g_tmp[:, :], g_tmp[:, :], GN_EPS, None, ALU.add).then_inc(gn_var.sem, 1)
                    dve.wait_ge(gn_rstd.sem, gn_rstd.after(b, n))
                    for k in range(CT):
                        last = dve.tensor_scalar(XN[:, k, :], X[:, k, :], gs[:, k, 0:1], g_rstd[:, k:k + 1],
                                                 ALU.subtract, ALU.mult)
                    last.then_inc(xn_ready.sem, 1)

                dve.wait_ge(x_loaded.sem, x_loaded.after(b, 1))
                group_norm(1)

                for m, (rows, bank) in enumerate([(P, 0), (XT, 2)]):
                    dve.wait_ge(xh_psum.sem, xh_psum.after(b, m + 1))
                    src = banks(bank)[0:rows, :].rearrange("p (h w) -> p h w", h=IMG)
                    acc = CONV[0:rows, m, :].rearrange("p (h w) -> p h w", h=IMG)
                    wc = COL["conv_w"]
                    last = dve.tensor_scalar(acc, src, wc[0:rows, 9 * m + 4:9 * m + 5],
                                             COL["conv_b"][0:rows, m:m + 1], ALU.mult, ALU.add)
                    for tap in [0, 1, 2, 3, 5, 6, 7, 8]:
                        link(last)
                        dy, dx = tap // 3 - 1, tap % 3 - 1
                        ys, xs_ = (max(0, -dy), IMG - max(0, dy)), (max(0, -dx), IMG - max(0, dx))
                        dst = acc[:, ys[0]:ys[1], xs_[0]:xs_[1]]
                        last = dve.scalar_tensor_tensor(
                            out=dst, in0=src[:, ys[0] + dy:ys[1] + dy, xs_[0] + dx:xs_[1] + dx],
                            scalar=wc[0:rows, 9 * m + tap:9 * m + tap + 1], in1=dst, op0=ALU.mult, op1=ALU.add)
                    last.then_inc(conv_done.sem, 1)

                dve.wait_ge(bc_hi.sem, bc_hi.after(b, 1))
                link(dve.tensor_tensor(REST[:, 0, :], banks(2), BCP[:, 0, :], ALU.subtract))
                link(dve.tensor_copy(BCP[:, 1, :], REST[:, 0, :]))
                link(dve.tensor_tensor(REST[:, 1, :], REST[:, 0, :], BCP[:, 1, :], ALU.subtract))
                dve.tensor_copy(BCP[:, 2, :], REST[:, 1, :]).then_inc(bc_split.sem, 1)

                def soft_series(s):
                    dve.wait_ge(soft_e.sem, soft_e.after(b, s + 1))
                    dve.tensor_scalar(MASK, SE, SMALL, None, ALU.is_lt)
                    link(dve.scalar_tensor_tensor(out=SQ3, in0=SE, scalar=-1.5, in1=SE, op0=ALU.add, op1=ALU.mult))
                    dve.scalar_tensor_tensor(out=SQ3, in0=SQ3, scalar=3.0, in1=SE, op0=ALU.add,
                                             op1=ALU.mult).then_inc(soft_q.sem, 1)

                def soft_pick(s):
                    dve.wait_ge(soft_ln.sem, soft_ln.after(b, s + 1))
                    dve.wait_ge(soft_q3.sem, soft_q3.after(b, s + 1))
                    dve.copy_predicated(DELTA[:, s % 2, :], MASK, SQ3).then_inc(soft_log.sem, 1)

                def scan(i):
                    s = i // NST
                    dve.wait_ge(da_ready.sem, da_ready.after(b, i + 1))
                    dve.wait_ge(dbu_ready.sem, dbu_ready.after(b, i + 1))
                    if i >= 2:
                        dve.wait_ge(hc_ready.sem, hc_ready.after(b, i - 1))
                    step = 1 if TILE_ORDER[s] < 3 else -1
                    dve.tensor_tensor_scan(HS[:, i % 2, ::step], DA[:, i % 3, ::step], DBU[:, i % 2, ::step],
                                           0.0, ALU.mult, ALU.add).then_inc(scan_done.sem, 1)

                def times_c(i):
                    dve.wait_ge(scan_done.sem, scan_done.after(b, i + 1))
                    dve.wait_ge(cslot_full.sem, cslot_full.after(b, i + 1))
                    if i >= 2:
                        dve.wait_ge(acc_done.sem, acc_done.after(b, i - 1))
                    dve.tensor_tensor(HC[:, i % 2, :], HS[:, i % 2, :], banks(2 + 2 * (i % 2)), ALU.mult
                                      ).then_inc(hc_ready.sem, 1)

                soft_series(0)
                soft_pick(0)
                for i in range(ITEMS):
                    s, n = divmod(i, NST)
                    scan(i)
                    if i:
                        times_c(i - 1)
                    if s < SEQ - 1 and n == 10:
                        soft_series(s + 1)
                    if s < SEQ - 1 and n == 12:
                        soft_pick(s + 1)
                times_c(ITEMS - 1)

                dve.wait_ge(y_psum.sem, y_psum.after(b, 1))
                for m, rows in ((0, P), (1, XT)):
                    last = dve.scalar_tensor_tensor(out=YF[0:rows, m, :], in0=U[0:rows, m, :],
                                                    scalar=skip_sum[0:rows, m:m + 1], in1=banks(2 * m)[0:rows, :],
                                                    op0=ALU.mult, op1=ALU.add)
                last.then_inc(yf_ready.sem, 1)
                dve.wait_ge(yf_ready.sem, yf_ready.after(b, 1))
                dve.wait_ge(mean_psum.sem, mean_psum.after(b, 1))
                for m, rows in ((0, P), (1, XT)):
                    last = dve.tensor_tensor(YF[0:rows, m, :], YF[0:rows, m, :], banks(4)[0:rows, :], ALU.subtract)
                last.then_inc(yc_ready.sem, 1)
                dve.wait_ge(rstd_ready.sem, rstd_ready.after(b, 1))
                for m, rows in ((0, P), (1, XT)):
                    last = dve.tensor_tensor(YF[0:rows, m, :], YF[0:rows, m, :], RSTD[0:rows, :], ALU.mult)
                link(last)
                for m, rows in ((0, P), (1, XT)):
                    last = dve.tensor_scalar(YF[0:rows, m, :], YF[0:rows, m, :], COL["norm_g"][0:rows, m:m + 1],
                                             COL["norm_b"][0:rows, m:m + 1], ALU.mult, ALU.add)
                link(last)
                for m, rows in ((0, P), (1, XT)):
                    last = dve.tensor_tensor(YF[0:rows, m, :], YF[0:rows, m, :], ZS[0:rows, m, :], ALU.mult)
                last.then_inc(yg_ready.sem, 1)
                dve.wait_ge(op_psum.sem, op_psum.after(b, 1))
                for m in range(CT):
                    last = dve.tensor_tensor(X[:, m, :], X[:, m, :], banks(2 * m), ALU.add)
                link(last)

                group_norm(2)
                for g in range(GROUPS):
                    for side in range(2):
                        dve.wait_ge(turn_psum.sem, turn_psum.after(b, 2 * g + side + 1))
                        dve.tensor_tensor(RT1, QKB[:, side, :], W["cos"][:, 0, :], ALU.mult)
                        link(dve.tensor_tensor(RT2, banks(4 + 2 * side), W["sin"][:, 0, :], ALU.mult))
                        dve.tensor_tensor(QKB[:, side, :], RT1, RT2, ALU.add).then_inc(rope_ready.sem, 1)
                        dve.wait_ge(rope_ready.sem, rope_ready.after(b, 2 * g + side + 1))
                    for c in range(4):
                        dve.wait_ge(rel_psum.sem, rel_psum.after(b, 4 * g + c + 1))
                        src = banks(2 * (c % 2))[2 * HD:3 * HD, :].rearrange("p (w j h) -> p j w h", w=8, j=HG)
                        qw = QX[2 * HD:3 * HD, :, :].rearrange("p j (h w) -> p j w h", h=IMG)
                        for j in range(HG):
                            last = dve.tensor_copy(qw[:, j, 8 * c:8 * c + 8, :], src[:, j, :, :])
                        last.then_inc(relw_saved.sem, 1)

                    def save_turned(k):
                        s = STEPS * g + k
                        qb, j = divmod(k, HG)
                        dve.wait_ge(pt_psum.sem, pt_psum.after(b, s + 1))
                        if QB * g + qb >= 2:
                            dve.wait_ge(o_psum.sem, o_psum.after(b, QB * g + qb - 1))
                        dve.tensor_copy(PT[:, qb % 2, j, :, :],
                                        banks(4).rearrange("p (t q) -> p t q", t=QB)).then_inc(pt_saved.sem, 1)

                    for k in range(STEPS):
                        s = STEPS * g + k
                        dve.wait_ge(s_psum.sem, s_psum.after(b, s + 1))
                        if s >= 4:
                            dve.wait_ge(exp_done.sem, exp_done.after(b, s - 3))
                        dve.tensor_reduce(neg_max[:, k % 4:k % 4 + 1], banks(2 * (k % 2)), AX_X, ALU.max,
                                          negate=True).then_inc(max_done.sem, 1)
                        if k and k % 2 == 1:
                            save_turned(k - 1)

                dve.wait_ge(exp_done.sem, exp_done.after(b, STEPS * GROUPS))
                dve.reciprocal(row_sum[:, :, :], row_sum[:, :, :]).then_inc(rs_ready.sem, 1)
                dve.wait_ge(rb_psum.sem, rb_psum.after(b, 1))
                dve.wait_ge(o_saved.sem, o_saved.after(b, QB * GROUPS))
                for g in range(GROUPS):
                    last = dve.tensor_tensor(OT[:, g, :], OT[:, g, :], banks(2 + 2 * g), ALU.mult)
                link(last)
                for g in range(GROUPS):
                    last = dve.tensor_scalar(OT[:, g, :], OT[:, g, :], COL["b_qkv"][:, 6 + g:7 + g], None, ALU.add)
                last.then_inc(on_ready.sem, 1)
                dve.wait_ge(pj_psum.sem, pj_psum.after(b, 1))
                for m in range(CT):
                    last = dve.scalar_tensor_tensor(out=OUT[:, m, :], in0=banks(2 * m), scalar=COL["b_proj"][:, m:m + 1],
                                                    in1=X[:, m, :], op0=ALU.add, op1=ALU.add)
                last.then_inc(out_ready.sem, 1)
                leave_image(dve, b)

        @block.scalar
        def _(act):
            act.wait_ge(consts.sem, 16 * N_CONST)
            act.wait_ge(prep.sem, 1)
            act.activation(a_neg[:, :], a_low[:, :], ACT.Exp).then_inc(a_exp, 1)
            act.wait_ge(a_exp, 1)
            act.mul(a_neg[:, :], a_neg[:, :], -1.0).then_inc(prep.sem, 1)
            act.wait_ge(prep.sem, 4)

            with act.Fori(0, B) as b:
                link = steps(act, act_step, b)

                def group_rstd(n):
                    act.wait_ge(gn_var.sem, gn_var.after(b, n))
                    link(act.activation(g_rstd[:, :], g_tmp[:, :], ACT.Ln))
                    act.activation(g_rstd[:, :], g_rstd[:, :], ACT.Exp, scale=-0.5).then_inc(gn_rstd.sem, 1)

                group_rstd(1)
                act.wait_ge(conv_done.sem, conv_done.after(b, 2))

                def by_column(ap):
                    return ap.rearrange("p (h w) -> p w h", h=IMG)

                def grid(ap):
                    return ap.rearrange("p (w h) -> p w h", h=IMG)

                act.activation(U[:, 0, :], CONV[:, 0, :], ACT.Silu)
                act.activation(U[0:XT, 1, :], CONV[0:XT, 1, :], ACT.Silu)
                act.activation(grid(U[XT:P, 1, :]), by_column(CONV[0:XT, 0, :]), ACT.Silu)
                act.activation(grid(U[0:XT, 2, :]), by_column(CONV[XT:P, 0, :]), ACT.Silu)
                act.activation(grid(U[XT:P, 2, :]), by_column(CONV[0:XT, 1, :]), ACT.Silu).then_inc(u_ready.sem, 1)
                act.wait_ge(z_psum.sem, z_psum.after(b, 1))
                act.activation(ZS[:, 0, :], banks(4), ACT.Silu)
                link(act.activation(ZS[0:XT, 1, :], banks(6)[0:XT, :], ACT.Silu))
                act.wait_ge(xdbl_psum.sem, xdbl_psum.after(b, 1))
                act.activation(BCP[:, 0, :], banks(2), ACT.Copy).then_inc(bc_hi.sem, 1)
                act.activation(DTS, banks(0), ACT.Copy).then_inc(dts_saved.sem, 1)

                slot = [0]

                def soft(s):
                    t = TILE_ORDER[s]
                    slot[0] += 1
                    act.wait_ge(bslot_full.sem, bslot_full.after(b, slot[0]))
                    bias = COL["dt_b"][:, t:t + 1]
                    if s:
                        act.wait_ge(delta_ready.sem, delta_ready.after(b, s))
                    link(act.activation(SE, banks(0), ACT.Abs, bias=bias))
                    act.activation(SR, banks(0), ACT.Relu, bias=bias).then_inc(bslot_free.sem, 1)
                    act.activation(SE, SE, ACT.Exp, scale=-1.0).then_inc(soft_e.sem, 1)
                    act.wait_ge(soft_e.sem, soft_e.after(b, s + 1))
                    act.activation(DELTA[:, s % 2, :], SE, ACT.Ln, bias=one[:, 0:1]).then_inc(soft_ln.sem, 1)

                def soft_third(s):
                    act.wait_ge(soft_q.sem, soft_q.after(b, s + 1))
                    act.activation(SQ3, SQ3, ACT.Copy, scale=1.0 / 3.0).then_inc(soft_q3.sem, 1)

                def decay(i):
                    s, n = divmod(i, NST)
                    if n == 0:
                        act.wait_ge(delta_ready.sem, delta_ready.after(b, s + 1))
                    if i >= 3:
                        act.wait_ge(scan_done.sem, scan_done.after(b, i - 2))
                    at = TILE_ORDER[s] * NST + n
                    act.activation(DA[:, i % 3, :], DELTA[:, s % 2, :], ACT.Exp, bias=a_inf[:, at:at + 1],
                                   scale=a_neg[:, at:at + 1]).then_inc(da_ready.sem, 1)

                soft(0)
                soft_third(0)
                for i in range(ITEMS):
                    s, n = divmod(i, NST)
                    slot[0] += 1
                    act.wait_ge(bslot_full.sem, bslot_full.after(b, slot[0]))
                    if i >= 2:
                        act.wait_ge(dbu_ready.sem, dbu_ready.after(b, i - 1))
                    act.activation(BSB[:, i % 2, :], banks(0), ACT.Copy).then_inc(bslot_free.sem, 1)
                    decay(i)
                    if n == NST // 2 and s < SEQ - 1:
                        soft(s + 1)
                    if n == 11 and s < SEQ - 1:
                        soft_third(s + 1)
                    pair, k = divmod(i, 2 * NST)
                    if (k == 1 and pair) or i == ITEMS - 1:
                        done = pair if i != ITEMS - 1 else pair + 1
                        act.wait_ge(acc_done.sem, acc_done.after(b, 2 * NST * done))
                        act.activation(YSB[:, done - 1, :], banks(6), ACT.Copy).then_inc(y_saved.sem, 1)

                act.wait_ge(yc_ready.sem, yc_ready.after(b, 1))
                act.activation(SQ[:, 0, :], YF[:, 0, :], ACT.Square)
                act.activation(SQ[0:XT, 1, :], YF[0:XT, 1, :], ACT.Square).then_inc(sq_ready.sem, 1)
                act.wait_ge(var_psum.sem, var_psum.after(b, 1))
                link(act.activation(RSTD, banks(6), ACT.Copy, bias=LN_EPS))
                link(act.activation(RSTD, RSTD, ACT.Ln))
                act.activation(RSTD, RSTD, ACT.Exp, scale=-0.5).then_inc(rstd_ready.sem, 1)

                group_rstd(2)
                for t in range(QB):
                    act.wait_ge(v_psum.sem, v_psum.after(b, t + 1))
                    act.activation(V[:, t, :], banks(t, 1)[:, 0:C], ACT.Copy).then_inc(v_saved.sem, 1)
                for g in range(GROUPS):
                    for side in range(2):
                        act.wait_ge(qk_psum.sem, qk_psum.after(b, 2 * g + side + 1))
                        if g:
                            loaded = (q_loaded, k_loaded)[side]
                            act.wait_ge(loaded.sem, loaded.after(b, HG * g))
                        bias = COL["b_qkv"][:, g:g + 1] if side == 0 else bk_scaled[:, g:g + 1]
                        act.activation(QKB[:, side, :], banks(2 * side), ACT.Identity, bias=bias,
                                       scale=1.0 if side == 0 else ATT_SCALE).then_inc(qk_saved.sem, 1)
                    for c in range(4):
                        act.wait_ge(rel_psum.sem, rel_psum.after(b, 4 * g + c + 1))
                        src = banks(2 * (c % 2))[HD:2 * HD, :].rearrange("p (h j w) -> p h j w", h=8, j=HG)
                        qh = QX[HD:2 * HD, :, :].rearrange("p j (h w) -> p h j w", h=IMG)
                        act.activation(qh[:, 8 * c:8 * c + 8, :, :], src, ACT.Copy).then_inc(relh_saved.sem, 1)

                    def save_turned(k):
                        s = STEPS * g + k
                        qb, j = divmod(k, HG)
                        act.wait_ge(pt_psum.sem, pt_psum.after(b, s + 1))
                        if QB * g + qb >= 2:
                            act.wait_ge(o_psum.sem, o_psum.after(b, QB * g + qb - 1))
                        act.activation(PT[:, qb % 2, j, :, :], banks(4).rearrange("p (t q) -> p t q", t=QB),
                                       ACT.Copy).then_inc(pt_saved.sem, 1)

                    def save_sums(qb):
                        n = QB * g + qb
                        act.wait_ge(o_psum.sem, o_psum.after(b, n + 1))
                        act.activation(OT[:, g, qb * P:(qb + 1) * P], banks(6 + qb % 2, 1)[:, 0:P],
                                       ACT.Copy).then_inc(o_saved.sem, 1)

                    for k in range(STEPS):
                        s = STEPS * g + k
                        qb, j = divmod(k, HG)
                        act.wait_ge(max_done.sem, max_done.after(b, s + 1))
                        if s >= 2:
                            act.wait_ge(pt_psum.sem, pt_psum.after(b, s - 1))
                        at = HG * g + j
                        act.activation(PR[:, k % 2, :], banks(2 * (k % 2)), ACT.Exp, bias=neg_max[:, k % 4:k % 4 + 1],
                                       accum_out=row_sum[:, qb, at:at + 1]).then_inc(exp_done.sem, 1)
                        if k and k % 2 == 0:
                            save_turned(k - 1)
                        if k % HG == 3 and k > HG:
                            save_sums(qb - 1)
                    save_turned(STEPS - 1)
                    save_sums(QB - 1)
                act.wait_ge(rt_psum.sem, rt_psum.after(b, 1))
                act.activation(RT[0:NH, :], banks(0)[0:NH, :], ACT.Copy).then_inc(rt_saved.sem, 1)
                leave_image(act, b)

        @block.gpsimd
        def _(pool):
            with pool.Fori(0, B) as b:
                def delta(s):
                    pool.wait_ge(soft_log.sem, soft_log.after(b, s + 1))
                    pool.tensor_tensor(DELTA[:, s % 2, :], DELTA[:, s % 2, :], SR, ALU.add
                                       ).then_inc(delta_ready.sem, 1)
                    pool.wait_ge(delta_ready.sem, delta_ready.after(b, s + 1))
                    pool.tensor_tensor(DU[:, s % 2, :], DELTA[:, s % 2, :], U[:, TILE_ORDER[s] % 3, :], ALU.mult
                                       ).then_inc(du_ready.sem, 1)

                delta(0)
                for i in range(ITEMS):
                    s, n = divmod(i, NST)
                    if n == 0:
                        pool.wait_ge(du_ready.sem, du_ready.after(b, s + 1))
                    pool.wait_ge(bslot_free.sem, bslot_free.after(b, i + 1 + dt_before(i)))
                    if i >= 2:
                        pool.wait_ge(scan_done.sem, scan_done.after(b, i - 1))
                    pool.tensor_tensor(DBU[:, i % 2, :], DU[:, s % 2, :], BSB[:, i % 2, :], ALU.mult
                                       ).then_inc(dbu_ready.sem, 1)
                    if s < SEQ - 1 and n == 13:
                        delta(s + 1)
                leave_image(pool, b)


def dt_before(i):
    s, n = divmod(i, NST)
    return 1 + s + (1 if n > NST // 2 and s < SEQ - 1 else 0)


def kernel(x, L0_conv_in_proj_w, L0_conv_conv_w, L0_conv_conv_b, L0_conv_x_proj_w, L0_conv_dt_projs_w,
           L0_conv_dt_projs_b, L0_conv_A_logs, L0_conv_Ds, L0_conv_out_norm_g, L0_conv_out_norm_b,
           L0_conv_out_proj_w, L1_conv_w_qkv, L1_conv_b_qkv, L1_conv_w_proj, L1_conv_b_proj,
           L1_conv_rel_pos_h, L1_conv_rel_pos_w):
    import ml_dtypes
    import numpy as np
    import concourse.bacc as bacc
    from concourse.bass_utils import run_bass_kernel_spmd

    f = np.float32

    def halves(v):
        v = np.asarray(v)
        o = np.zeros((P, 2) + v.shape[1:], f)
        o[:, 0] = v[:P]
        o[:XT, 1] = v[P:]
        return o

    def tiles(v):
        return np.ascontiguousarray(np.asarray(v).reshape(-1, P).T)

    mats, cols = {}, {}
    mats["w_in"] = np.asarray(L0_conv_in_proj_w).T
    xp = np.asarray(L0_conv_x_proj_w)
    w = np.zeros((2, DI, 2 * P), f)
    for k in range(DIRS):
        order = k % 2
        w[order, :, 32 * k:32 * k + RANK] = xp[k, :RANK].T
        for c in range(2):
            at = P + 64 * (k // 2) + 32 * c + NST * (k % 2)
            w[order, :, at:at + NST] = xp[k, RANK + NST * c:RANK + NST * (c + 1)].T
    mats["w_xdbl"] = np.concatenate([w[0], w[1]])
    wd = np.zeros((P, DIRS * DI), f)
    for k in range(DIRS):
        wd[32 * k:32 * k + RANK, DI * k:DI * (k + 1)] = np.asarray(L0_conv_dt_projs_w)[k].T
    mats["w_dt"] = wd
    wo = np.zeros((2 * P, C), f)
    wo[:DI] = np.asarray(L0_conv_out_proj_w).T
    mats["w_out"] = wo
    mats["w_qkv"] = np.asarray(L1_conv_w_qkv)
    mats["w_proj"] = np.asarray(L1_conv_w_proj)
    ch = np.arange(C)
    mats["group_mean"] = (ch[:, None] // 12 == ch[None, :] // 12) / f(12)
    freqs = (1.0 / np.power(f(10000.0), np.arange(0, HD, 4, dtype=f) / f(HD))).astype(f)
    tok = np.arange(L)
    ang = np.concatenate([(tok % IMG).astype(f)[:, None] * freqs, (tok // IMG).astype(f)[:, None] * freqs], 1)
    rows = (np.arange(P) % HD) // 2
    mats["cos"] = np.cos(ang).T[rows]
    mats["sin"] = np.sin(ang).T[rows]
    mats["ident"] = np.eye(P)
    mats["to_low"] = np.eye(P, k=-XT)
    mats["to_high"] = np.eye(P, k=XT)
    turn = np.zeros((P, P), f)
    for i in range(0, P, 2):
        turn[i + 1, i] = -1.0
        turn[i, i + 1] = 1.0
    mats["turn"] = turn
    mats["chan_mean"] = np.full((P, P), 1.0 / DI)
    hr = np.zeros((NH, C), f)
    hr[ch // HD, ch] = 1.0
    mats["head_rows"] = hr
    mats["rel_h"] = np.asarray(L1_conv_rel_pos_h)[:REL][::-1].T
    mats["rel_w"] = np.asarray(L1_conv_rel_pos_w)[:REL][::-1].T

    cols["conv_w"] = halves(np.asarray(L0_conv_conv_w).reshape(DI, 9)).reshape(P, 18)
    cols["conv_b"] = halves(L0_conv_conv_b)
    cols["dt_b"] = tiles(np.asarray(L0_conv_dt_projs_b).reshape(-1))
    cols["a_log"] = np.asarray(L0_conv_A_logs).reshape(SEQ, P, NST).transpose(1, 0, 2).reshape(P, SEQ * NST)
    cols["skip"] = halves(np.asarray(L0_conv_Ds).reshape(DIRS, DI).T).reshape(P, 2 * DIRS)
    cols["norm_g"] = halves(L0_conv_out_norm_g)
    cols["norm_b"] = halves(L0_conv_out_norm_b)
    cols["b_qkv"] = tiles(L1_conv_b_qkv)
    cols["b_proj"] = tiles(L1_conv_b_proj)

    sel = np.zeros((3, 2, NST, 3, NST, P), f)
    for n in range(NST):
        sel[:, 0, n, 0, n, :] = 1
        sel[:, 0, n, 1, n, :XT] = 1
        sel[:, 1, n, 1, n, XT:] = 1
        sel[:, 1, n, 2, n, :] = 1
    sel = sel.reshape(3 * 2 * NST, 3 * NST, P).astype(ml_dtypes.bfloat16)
    onehot = np.zeros((2 * IMG, L), f)
    onehot[tok // IMG, tok] = 1
    onehot[IMG + tok % IMG, tok] = 1
    xt = np.ascontiguousarray(np.asarray(x).reshape(B, L, C).transpose(0, 2, 1))

    nc = bacc.Bacc("TRN2", target_bir_lowering=False, num_devices=1)
    arrays = {}

    def given(name, a, dtype=f):
        a = np.ascontiguousarray(a, dtype)
        arrays[name] = a
        return nc.dram_tensor(name, a.shape, mybir.dt.from_np(a.dtype), kind="ExternalInput").ap()

    x_ap = given("x_in", xt)
    mat_aps = {k: given(k + "_in", v) for k, v in mats.items()}
    col_aps = {k: given(k + "_in", v) for k, v in cols.items()}
    sel_ap = given("sel_in", sel, ml_dtypes.bfloat16)
    onehot_ap = given("onehot_in", onehot)
    out_ap = nc.dram_tensor("out_t", (B, C, L), F32, kind="ExternalOutput").ap()
    build(nc, x_ap, mat_aps, col_aps, sel_ap, onehot_ap, out_ap)
    r = run_bass_kernel_spmd(nc, [arrays], core_ids=[0])
    got = np.asarray(r.results[0]["out_t"])
    return np.ascontiguousarray(got.transpose(0, 2, 1)).reshape(B, IMG, IMG, C)
```

```python
from contextlib import ExitStack

import concourse.bass as bass
from concourse import mybir

P = 128
B, IMG, C = 4, 32, 384
L = IMG * IMG
CT = C // P
HALF = L // 2
DI, NST, RANK, DIRS = 192, 16, 24, 4
SEQ = DIRS * DI // P
XT = 64
ITEMS = SEQ * NST
NH, HD = 12, 32
HG = P // HD
GROUPS = NH // HG
QB = L // P
STEPS = QB * HG
REL = 2 * IMG - 1
ATT_SCALE = float(HD) ** -0.5
GN_EPS = 1e-5
LN_EPS = 1e-5
SMALL = 2.0 ** -7
DT_AT = 7
C_LAG, ACC_LAG = 2, 4
A_LOG_MAX = 80.0
TILE_ORDER = [0, 3, 1, 4, 2, 5]

F32 = mybir.dt.float32
BF16 = mybir.dt.bfloat16
U8 = mybir.dt.uint8
ALU = mybir.AluOpType
ACT = mybir.ActivationFunctionType
AX_X = mybir.AxisListType.X

KEPT = {
    "group_mean": (3 * P, C), "ident": (P, P), "to_low": (P, P), "to_high": (P, P), "turn": (P, P),
    "chan_mean": (P, P), "head_rows": (NH, C), "rel_h": (P, REL * HG), "rel_w": (P, REL * HG),
}
SCAN_MATS = {"w_in": (3 * P, C), "w_xdbl": (3 * P, 2 * P), "w_dt": (P, SEQ * P)}
ATT_MATS = {"w_qkv": (3 * P, 3 * C), "cos": (P, L), "sin": (P, L)}
TAIL_MATS = {"w_out": (2 * P, C), "w_proj": (3 * P, C)}
COLS = {
    "conv_w": 2 * 9, "conv_b": 2, "dt_b": SEQ, "a_log": SEQ * NST, "skip": 2 * DIRS,
    "norm_g": 2, "norm_b": 2, "b_qkv": 9, "b_proj": 3,
}


class Signal:

    def __init__(self, sem, per_image, unit=1):
        self.sem, self.per_image, self.unit = sem, per_image, unit

    def after(self, b, n):
        return n * self.unit


def build(nc, x, mats, cols, sel_in, onehot, out):
    ctx = ExitStack()
    with ctx:
        def sb(name, shape, dt=F32):
            return ctx.enter_context(nc.sbuf_tensor(name, shape, dt))

        def signal(name, per_image, unit=1):
            return Signal(ctx.enter_context(nc.semaphore(name)), per_image, unit)

        X = sb("residual", [P, CT, L])
        XN = sb("normed", [P, CT, L])
        W = {}
        for name, (rows, width) in (KEPT | TAIL_MATS).items():
            W[name] = sb(name, [min(rows, P), max(rows // P, 1), width])
        COL = {name: sb(name, [P, width]) for name, width in COLS.items()}
        one = sb("one", [P, 1])
        eps = sb("eps", [P, 1])
        a_neg = sb("a_neg", [P, SEQ * NST])
        a_low = sb("a_low", [P, SEQ * NST])
        a_inf = sb("a_inf", [P, SEQ * NST])
        skip_sum = sb("skip_sum", [P, 2])
        bk_scaled = sb("bk_scaled", [P, GROUPS])
        bn = sb("bn", [P, CT, 2, 6])
        mv = sb("mv", [P, CT, 2])
        gs = sb("gs", [P, CT, 2])
        g_tmp = sb("g_tmp", [P, CT])
        g_rstd = sb("g_rstd", [P, CT])
        neg_max = sb("neg_max", [P, 4])
        row_sum = sb("row_sum", [P, QB, NH])
        M0 = -(-max(sum(max(rows // P, 1) * width for rows, width in ATT_MATS.values()),
                    sum(max(rows // P, 1) * width for rows, width in SCAN_MATS.values()) + 3 * NST * P // 2) // HALF)
        arena = sb("arena", [P, M0 * HALF + 33 * L])
        PS = ctx.enter_context(nc.psum_tensor("PS", [P, 8 * HALF], F32))

        def unit(k, n=1):
            return arena[:, k * L:(k + n) * L]

        def units(k, n):
            return unit(k, n).rearrange("p (n l) -> p n l", n=n)

        def banks(k, n=2):
            return PS[:, k * HALF:(k + n) * HALF]

        def place_mats(which, at):
            for name, (rows, width) in which.items():
                k = max(rows // P, 1)
                W[name] = arena[:, at:at + k * width].rearrange("p (k c) -> p k c", k=k)
                at += k * width
            return at

        at = place_mats(SCAN_MATS, 0)
        SEL = arena[0:3 * 2 * NST, at:at + 3 * NST * P // 2].bitcast(BF16).rearrange("p (s c) -> p s c", c=P)
        place_mats(ATT_MATS, 0)

        def from_mats(k, n=1):
            o = M0 * HALF + k * L
            return arena[:, o:o + n * L].rearrange("p (n l) -> p n l", n=n)

        U, YSB, ZS, DTS = from_mats(0, 3), from_mats(3, 3), from_mats(6, 2), from_mats(8)[:, 0, :]
        BCS = from_mats(9, 2).rearrange("p n l -> p (n l)").bitcast(BF16).rearrange("p (g l) -> p g l", g=4)
        DELTA, DU = from_mats(11, 2), from_mats(13, 2)
        SE, SQ3, SR = [from_mats(15 + k)[:, 0, :] for k in range(3)]
        MASK = from_mats(18)[:, 0, 0:L // 4].bitcast(U8)
        R3 = 3
        HS, DA, BSB, DBU, HC = (from_mats(19, 2), from_mats(21, 3), from_mats(24, R3), from_mats(27, R3),
                                from_mats(30, R3))
        CONV = from_mats(19, 2)
        BCP = from_mats(21, 2).rearrange("p n l -> p (n l)").bitcast(BF16)[:, 0:3 * L].rearrange(
            "p (a l) -> p a l", a=3)
        REST = from_mats(23, 2)
        YF, SQ, RSTD = from_mats(11, 2), from_mats(13, 2), from_mats(15)[:, 0, :]
        QX, KX = from_mats(19, HG), from_mats(23, HG)
        V = from_mats(0, 3).rearrange("p n l -> p (n l)").rearrange("p (t c) -> p t c", t=QB)
        OT = from_mats(3, 3)
        PR = from_mats(6, 2)
        QKC, RELC = from_mats(8, 2), from_mats(31, 2)
        PT = from_mats(11, 8).rearrange("p n l -> p (n l)").rearrange("p (s j t q) -> p s j t q", s=2, j=HG, t=QB)
        OUT = from_mats(11, 3)
        RAW, RT1, RT2 = [from_mats(27 + k)[:, 0, :].rearrange("p (s l) -> p s l", s=2) for k in range(3)]
        RT = from_mats(30)[:, 0, :]

        consts = signal("consts_loaded", 0, 16)
        prep = signal("consts_prepared", 0)
        a_exp = ctx.enter_context(nc.semaphore("a_exp"))
        image_done = ctx.enter_context(nc.semaphore("image_done"))
        clearing = ctx.enter_context(nc.semaphore("clearing"))
        image_open = ctx.enter_context(nc.semaphore("image_open"))
        first_x = signal("first_x", 0, 16)
        x_loaded = signal("x_loaded", 1, 16)
        next_loaded = signal("next_loaded", 5, 16)
        att_loaded = signal("att_loaded", len(ATT_MATS), 16)
        gn_stats = signal("gn_stats", 2)
        gn_psum = signal("gn_psum", 2)
        gn_var = signal("gn_var", 2)
        gn_rstd = signal("gn_rstd", 2)
        xn_ready = signal("xn_ready", 2)
        xh_psum = signal("xh_psum", 2)
        z_psum = signal("z_psum", 1)
        conv_done = signal("conv_done", 2)
        u_ready = signal("u_ready", 1)
        xdbl_psum = signal("xdbl_psum", 1)
        dts_saved = signal("dts_saved", 1)
        bc_hi = signal("bc_hi", 1)
        bc_split = signal("bc_split", 1)
        bcs_loaded = signal("bcs_loaded", 12, 16)
        bslot_full = signal("bslot_full", ITEMS + SEQ)
        bslot_free = signal("bslot_free", ITEMS + SEQ)
        cslot_full = signal("cslot_full", ITEMS)
        soft_e = signal("soft_e", SEQ)
        soft_ln = signal("soft_ln", SEQ)
        soft_q = signal("soft_q", SEQ)
        soft_q2 = signal("soft_q2", SEQ)
        soft_q3 = signal("soft_q3", SEQ)
        soft_log = signal("soft_log", SEQ)
        delta_ready = signal("delta_ready", SEQ)
        du_ready = signal("du_ready", SEQ)
        da_ready = signal("da_ready", ITEMS)
        bsb_ready = signal("bsb_ready", ITEMS)
        dbu_ready = signal("dbu_ready", ITEMS)
        scan_done = signal("scan_done", ITEMS)
        hc_ready = signal("hc_ready", ITEMS)
        acc_done = signal("acc_done", ITEMS)
        y_saved = signal("y_saved", 3)
        y_psum = signal("y_psum", 2)
        yf_ready = signal("yf_ready", 2)
        mean_psum = signal("mean_psum", 2)
        yc_ready = signal("yc_ready", 2)
        sq_ready = signal("sq_ready", 2)
        var_psum = signal("var_psum", 2)
        rstd_ready = signal("rstd_ready", 2)
        yg_ready = signal("yg_ready", 2)
        op_psum = signal("op_psum", 2)
        v_psum = signal("v_psum", QB)
        v_saved = signal("v_saved", QB)
        onehot_loaded = signal("onehot_loaded", HG, 16)
        proj_psum = signal("proj_psum", 4 * GROUPS)
        raw_saved = signal("raw_saved", 4 * GROUPS)
        cos_done = signal("cos_done", 4 * GROUPS)
        turn_psum = signal("turn_psum", 4 * GROUPS)
        sin_done = signal("sin_done", 4 * GROUPS)
        rope_ready = signal("rope_ready", 4 * GROUPS)
        rel_psum = signal("rel_psum", 4 * GROUPS)
        rel_saved = signal("rel_saved", 4 * GROUPS)
        head_loaded = [signal(f"head{j}_loaded", 4 * GROUPS, 16) for j in range(HG)]
        s_psum = signal("s_psum", STEPS * GROUPS)
        max_done = signal("max_done", STEPS * GROUPS)
        exp_done = signal("exp_done", STEPS * GROUPS)
        pt_psum = signal("pt_psum", STEPS * GROUPS)
        pt_saved = signal("pt_saved", STEPS * GROUPS)
        o_psum = signal("o_psum", QB * GROUPS)
        o_saved = signal("o_saved", QB * GROUPS)
        rs_ready = signal("rs_ready", 1)
        rt_psum = signal("rt_psum", 1)
        rt_saved = signal("rt_saved", 1)
        rb_psum = signal("rb_psum", 1)
        on_ready = signal("on_ready", 1)
        pj_psum = signal("pj_psum", 1)
        out_ready = signal("out_ready", 1)
        out_stored = signal("out_stored", 1, 16)
        dve_step = signal("dve_step", 0)
        act_step = signal("act_step", 0)

        def steps(eng, sig, b):
            count = [0]

            def link(ins):
                count[0] += 1
                ins.then_inc(sig.sem, 1)
                eng.wait_ge(sig.sem, sig.after(b, count[0]))
            return link

        first, last_sem = x_loaded.sem, act_step.sem
        per_image = range(first.num, last_sem.num + 1)

        def leave_image(eng, b):
            eng.sem_inc(image_done, 1)
            eng.wait_ge(image_open, b + 1)

        N_CONST = len(KEPT) + len(TAIL_MATS) + len(COLS)

        JOBS = [("proj", 0), ("proj", 1), ("turn", 0), ("turn", 1), ("proj", 2), ("proj", 3),
                ("rel", 0), ("rel", 1), ("rel", 2), ("rel", 3), ("turn", 2), ("turn", 3)]
        JOB_AT = {2 * m + 2: m for m in range(len(JOBS))}

        block = ctx.enter_context(nc.Block())

        @block.sync
        def _(sp):
            def load_mats(which, sig):
                for name in which:
                    rows = which[name][0]
                    sp.dma_start(W[name], mats[name].rearrange("(k p) c -> p k c", k=max(rows // P, 1))
                                 ).then_inc(sig.sem, 16)

            def load_scan(i, sig):
                sp.dma_start(XN[:, :, :], x[bass.ds(i, 1), :, :].rearrange("o (k p) l -> p (o k) l", p=P)
                             ).then_inc(sig.sem, 16)
                load_mats(SCAN_MATS, sig)
                sp.dma_start(SEL, sel_in).then_inc(sig.sem, 16)

            load_scan(0, first_x)
            for name, (rows, width) in (KEPT | TAIL_MATS).items():
                k = max(rows // P, 1)
                sp.dma_start(W[name][:, :, :], mats[name].rearrange("(k p) c -> p k c", k=k)).then_inc(consts.sem, 16)
            for name in COLS:
                sp.dma_start(COL[name][:, :], cols[name]).then_inc(consts.sem, 16)
            with sp.Fori(0, B) as b:
                sp.dma_start(X[:, :, :], x[bass.ds(b, 1), :, :].rearrange("o (k p) l -> p (o k) l", p=P)
                             ).then_inc(x_loaded.sem, 16)
                sp.wait_ge(bc_split.sem, bc_split.after(b, 1))
                for part in range(3):
                    for g in range(4):
                        sp.dma_start(BCS[32 * part:32 * part + 32, g, :], BCP[32 * g:32 * g + 32, part, :]
                                     ).then_inc(bcs_loaded.sem, 16)
                sp.wait_ge(acc_done.sem, acc_done.after(b, ITEMS))
                load_mats(ATT_MATS, att_loaded)
                for j in range(HG):
                    sp.dma_start(KX[HD:3 * HD, j, :], onehot).then_inc(onehot_loaded.sem, 16)
                for g in range(GROUPS):
                    sp.wait_ge(rope_ready.sem, rope_ready.after(b, 4 * g + 4))
                    sp.wait_ge(rel_saved.sem, rel_saved.after(b, 4 * g + 4))
                    for j in range(HG):
                        if g:
                            sp.wait_ge(s_psum.sem, s_psum.after(b, STEPS * g - HG + j + 1))
                        rows = slice(HD * j, HD * j + HD)
                        for dst, src in ((QX[0:HD, j, :], QKC[rows, 0, :]), (QX[HD:2 * HD, j, :], RELC[j::HG, 0, :]),
                                         (QX[2 * HD:3 * HD, j, :], RELC[j::HG, 1, :]), (KX[0:HD, j, :], QKC[rows, 1, :])):
                            sp.dma_start(dst, src).then_inc(head_loaded[j].sem, 16)
                load_scan((b + 1) % B, next_loaded)
                sp.wait_ge(out_ready.sem, out_ready.after(b, 1))
                sp.dma_start(out[bass.ds(b, 1), :, :].rearrange("o (k p) l -> p (o k) l", p=P), OUT[:, :, :]
                             ).then_inc(out_stored.sem, 16)
                sp.wait_ge(out_stored.sem, out_stored.after(b, 1))
                sp.wait_ge(next_loaded.sem, next_loaded.after(b, 5))
                sp.wait_ge(image_done, 4 * b + 4)
                sp.sem_inc(clearing, 1)
                sp.sem_clear(per_image)
                sp.sem_inc(image_open, 1)

        @block.tensor
        def _(pe):
            pe.wait_ge(consts.sem, 16 * N_CONST)
            pe.wait_ge(prep.sem, 4)
            pe.wait_ge(first_x.sem, first_x.after(0, 5))

            def half_product(dst, h, pairs):
                for k, (lhs, rhs) in enumerate(pairs):
                    last = pe.matmul(dst, lhs, rhs(h), start=(k == 0), stop=(k == len(pairs) - 1))
                return last

            def product(dst, pairs):
                for h in range(2):
                    for k, (lhs, rhs) in enumerate(pairs):
                        last = pe.matmul(dst[:, h * HALF:(h + 1) * HALF], lhs, rhs(h),
                                         start=(k == 0), stop=(k == len(pairs) - 1))
                return last

            def flat(ap):
                return lambda h: ap[:, h * HALF:(h + 1) * HALF]

            def turned(ap):
                return lambda h: ap.rearrange("p (w h) -> p h w", h=IMG)[:, h * (IMG // 2):(h + 1) * (IMG // 2), :]

            def group_stats(b, n):
                pe.wait_ge(gn_stats.sem, gn_stats.after(b, n))
                for m in range(CT):
                    for k in range(CT):
                        last = pe.matmul(PS[:, 6 * HALF + 2 * m:6 * HALF + 2 * m + 2],
                                         W["group_mean"][:, k, m * P:(m + 1) * P], mv[:, k, :],
                                         start=(k == 0), stop=(k == CT - 1), skip_group_check=True)
                last.then_inc(gn_psum.sem, 1)

            with pe.Fori(0, B) as b:
                group_stats(b, 1)
                pe.wait_ge(xn_ready.sem, xn_ready.after(b, 1))
                xn = [flat(XN[:, k, :]) for k in range(CT)]
                for m, (c0, rows, bank) in enumerate([(0, P, 0), (P, XT, 2), (DI, P, 4), (DI + P, XT, 6)]):
                    last = product(banks(bank)[0:rows, :],
                                   [(W["w_in"][:, k, c0:c0 + rows], xn[k]) for k in range(CT)])
                    if m < 2:
                        last.then_inc(xh_psum.sem, 1)
                last.then_inc(z_psum.sem, 1)
                pe.wait_ge(u_ready.sem, u_ready.after(b, 1))
                us = [flat(U[:, k, :]) for k in range(3)]
                product(banks(0), [(W["w_xdbl"][:, k, 0:P], us[k]) for k in range(3)])
                product(banks(2), [(W["w_xdbl"][:, k, P:2 * P], us[k]) for k in range(3)]
                        ).then_inc(xdbl_psum.sem, 1)

                slot = [0]

                def b_slot():
                    if slot[0]:
                        pe.wait_ge(bslot_free.sem, bslot_free.after(b, slot[0]))
                    slot[0] += 1

                def dt_product(s):
                    b_slot()
                    t = TILE_ORDER[s]
                    product(banks(0), [(W["w_dt"][:, 0, t * P:(t + 1) * P], flat(DTS))]
                            ).then_inc(bslot_full.sem, 1)

                def broadcast(dst, i, c):
                    s, n = divmod(i, NST)
                    t = TILE_ORDER[s]
                    return product(dst, [(SEL[:, (t % 3) * NST + n, :], flat(BCS[0:96, 2 * (t // 3) + c, :]))])

                def c_product(i):
                    if i >= 2:
                        pe.wait_ge(hc_ready.sem, hc_ready.after(b, i - 1))
                    broadcast(banks(2 + 2 * (i % 2)), i, 1).then_inc(cslot_full.sem, 1)

                def accumulate(i):
                    pe.wait_ge(hc_ready.sem, hc_ready.after(b, i + 1))
                    pair, k = divmod(i, 2 * NST)
                    if k == 0 and pair:
                        pe.wait_ge(y_saved.sem, y_saved.after(b, pair))
                    for h in range(2):
                        last = pe.matmul(banks(6)[:, h * HALF:(h + 1) * HALF], W["ident"][:, 0, :],
                                         HC[:, i % R3, h * HALF:(h + 1) * HALF],
                                         start=(k == 0), stop=(k == 2 * NST - 1), skip_group_check=True)
                    last.then_inc(acc_done.sem, 1)

                pe.wait_ge(dts_saved.sem, dts_saved.after(b, 1))
                pe.wait_ge(bc_split.sem, bc_split.after(b, 1))
                dt_product(0)
                pe.wait_ge(bcs_loaded.sem, bcs_loaded.after(b, 12))
                for i in range(ITEMS):
                    s, n = divmod(i, NST)
                    b_slot()
                    broadcast(banks(0), i, 0).then_inc(bslot_full.sem, 1)
                    if n == DT_AT and s < SEQ - 1:
                        dt_product(s + 1)
                    if i >= C_LAG:
                        c_product(i - C_LAG)
                    if i >= ACC_LAG:
                        accumulate(i - ACC_LAG)
                for i in range(ITEMS, ITEMS + ACC_LAG):
                    if i - C_LAG < ITEMS:
                        c_product(i - C_LAG)
                    accumulate(i - ACC_LAG)

                def bank(k, h):
                    return banks(2 * k + h, 1)

                pe.wait_ge(y_saved.sem, y_saved.after(b, 3))
                low, high, idn = W["to_low"][:, 0, :], W["to_high"][:, 0, :], W["ident"][:, 0, :]
                for h in range(2):
                    half_product(bank(0, h), h, [(idn, flat(YSB[:, 0, :])), (low, turned(YSB[:, 1, :])),
                                                 (high, turned(YSB[:, 2, :]))])
                    half_product(bank(1, h)[0:XT, :], h, [(idn[:, 0:XT], flat(YSB[:, 1, :])),
                                                          (low[:, 0:XT], turned(YSB[:, 2, :]))]
                                 ).then_inc(y_psum.sem, 1)
                cm = W["chan_mean"][:, 0, :]
                for h in range(2):
                    pe.wait_ge(yf_ready.sem, yf_ready.after(b, h + 1))
                    half_product(bank(2, h), h, [(cm, flat(YF[:, 0, :])), (cm[0:XT, :], flat(YF[0:XT, 1, :]))]
                                 ).then_inc(mean_psum.sem, 1)
                for h in range(2):
                    pe.wait_ge(sq_ready.sem, sq_ready.after(b, h + 1))
                    half_product(bank(3, h), h, [(cm, flat(SQ[:, 0, :])), (cm[0:XT, :], flat(SQ[0:XT, 1, :]))]
                                 ).then_inc(var_psum.sem, 1)
                for h in range(2):
                    pe.wait_ge(yg_ready.sem, yg_ready.after(b, h + 1))
                    for m in range(CT):
                        last = half_product(bank(m, h), h, [
                            (W["w_out"][:, 0, m * P:(m + 1) * P], flat(YF[:, 0, :])),
                            (W["w_out"][0:XT, 1, m * P:(m + 1) * P], flat(YF[0:XT, 1, :]))])
                    last.then_inc(op_psum.sem, 1)

                group_stats(b, 2)
                pe.wait_ge(xn_ready.sem, xn_ready.after(b, 2))
                pe.wait_ge(att_loaded.sem, att_loaded.after(b, len(ATT_MATS)))

                def values(t):
                    if t >= 4:
                        pe.wait_ge(v_saved.sem, v_saved.after(b, t - 3))
                    for k in range(CT):
                        last = pe.matmul(banks(t % 4, 1)[:, 0:C], XN[:, k, t * P:(t + 1) * P],
                                         W["w_qkv"][:, k, 2 * C:3 * C], start=(k == 0), stop=(k == CT - 1))
                    last.then_inc(v_psum.sem, 1)

                def job(g, m):
                    kind, n = JOBS[m]
                    prev = JOBS[m - 1]
                    if g or m:
                        sig = {"proj": raw_saved, "turn": sin_done, "rel": rel_saved}[prev[0]]
                        pe.wait_ge(sig.sem, sig.after(b, 4 * (g if m else g - 1) + prev[1] + 1))
                    dst = banks(7, 1)
                    part, h = divmod(n, 2)
                    if kind == "proj":
                        half_product(dst, h, [(W["w_qkv"][:, k, part * C + g * P:part * C + (g + 1) * P], xn[k])
                                              for k in range(CT)]).then_inc(proj_psum.sem, 1)
                    elif kind == "turn":
                        pe.wait_ge(raw_saved.sem, raw_saved.after(b, 4 * g + n + 1))
                        pe.matmul(dst, W["turn"][:, 0, :], RAW[:, h, :], start=True, stop=True
                                  ).then_inc(turn_psum.sem, 1)
                    else:
                        pe.wait_ge(rope_ready.sem, rope_ready.after(b, 4 * g + 2))
                        grid = QKC[:, 0, :].rearrange("p (h w) -> p h w", h=IMG)
                        mat = W[("rel_h", "rel_w")[part]][:, 0, :]
                        for r in range(IMG // 2):
                            at = h * (IMG // 2) + r
                            last = pe.matmul(dst[:, r * IMG:(r + 1) * IMG], mat[:, HG * (IMG - 1 - at):HG * (REL - at)],
                                             grid[:, at, :] if part == 0 else grid[:, :, at],
                                             start=True, stop=True, skip_group_check=True)
                        last.then_inc(rel_psum.sem, 1)

                def scores(s):
                    g, k = divmod(s, STEPS)
                    qb, j = divmod(k, HG)
                    if qb == 0:
                        pe.wait_ge(head_loaded[j].sem, head_loaded[j].after(b, 4 * (g + 1)))
                    if s >= 2:
                        pe.wait_ge(exp_done.sem, exp_done.after(b, s - 1))
                    product(banks(2 * (s % 2)), [(QX[0:3 * HD, j, qb * P:(qb + 1) * P], flat(KX[0:3 * HD, j, :]))]
                            ).then_inc(s_psum.sem, 1)

                def turn_probs(s):
                    pe.wait_ge(exp_done.sem, exp_done.after(b, s + 1))
                    if s:
                        pe.wait_ge(pt_saved.sem, pt_saved.after(b, s))
                    for t in range(QB):
                        last = pe.transpose(banks(4)[:, t * P:(t + 1) * P], PR[:, s % 2, t * P:(t + 1) * P], idn)
                    last.then_inc(pt_psum.sem, 1)

                def weigh(n):
                    g = n // QB
                    pe.wait_ge(pt_saved.sem, pt_saved.after(b, HG * (n + 1)))
                    if n:
                        pe.wait_ge(o_saved.sem, o_saved.after(b, n))
                    for t in range(QB):
                        for j in range(HG):
                            head = HG * g + j
                            last = pe.matmul(banks(6, 1)[HD * j:HD * j + HD, (n % 2) * P:(n % 2 + 1) * P],
                                             V[:, t, head * HD:(head + 1) * HD], PT[:, n % 2, j, t, :],
                                             start=(t == 0), stop=(t == QB - 1), skip_group_check=True)
                    last.then_inc(o_psum.sem, 1)

                for m in range(len(JOBS)):
                    job(0, m)
                    if m < QB:
                        values(m)
                pe.wait_ge(v_saved.sem, v_saved.after(b, QB))
                pe.wait_ge(onehot_loaded.sem, onehot_loaded.after(b, HG))
                scores(0)
                for s in range(STEPS * GROUPS):
                    g, k = divmod(s, STEPS)
                    if s + 1 < STEPS * GROUPS:
                        scores(s + 1)
                    if g + 1 < GROUPS and k in JOB_AT:
                        job(g + 1, JOB_AT[k])
                    if s % HG == 1 and s > HG:
                        weigh(s // HG - 1)
                    turn_probs(s)
                weigh(QB * GROUPS - 1)

                pe.wait_ge(rs_ready.sem, rs_ready.after(b, 1))
                for t in range(QB):
                    last = pe.transpose(banks(0)[0:NH, t * P:(t + 1) * P], row_sum[:, t, :], idn)
                last.then_inc(rt_psum.sem, 1)
                pe.wait_ge(rt_saved.sem, rt_saved.after(b, 1))
                for g in range(GROUPS):
                    last = product(banks(2 + 2 * g), [(W["head_rows"][0:NH, 0, g * P:(g + 1) * P], flat(RT[0:NH, :]))])
                last.then_inc(rb_psum.sem, 1)
                pe.wait_ge(on_ready.sem, on_ready.after(b, 1))
                for m in range(CT):
                    last = product(banks(2 * m), [(W["w_proj"][:, k, m * P:(m + 1) * P], flat(OT[:, k, :]))
                                                  for k in range(CT)])
                last.then_inc(pj_psum.sem, 1)
                leave_image(pe, b)

        @block.vector
        def _(dve):
            dve.memset(one[:, :], 1.0)
            dve.memset(eps[:, :], LN_EPS)
            dve.wait_ge(consts.sem, 16 * N_CONST)
            dve.tensor_scalar(a_inf[:, :], COL["a_log"][:, :], A_LOG_MAX, -200.0, ALU.is_gt, ALU.mult)
            dve.tensor_scalar(a_low[:, :], COL["a_log"][:, :], A_LOG_MAX, None, ALU.min).then_inc(prep.sem, 1)
            sk = COL["skip"][:, :].rearrange("p (m k) -> p m k", m=2)
            dve.tensor_reduce(skip_sum[:, :], sk, AX_X, ALU.add).then_inc(prep.sem, 1)
            dve.tensor_scalar(bk_scaled[:, :], COL["b_qkv"][:, 3:6], ATT_SCALE, None, ALU.mult).then_inc(prep.sem, 1)
            dve.wait_ge(prep.sem, 4)
            dve.wait_ge(first_x.sem, first_x.after(0, 5))

            with dve.Fori(0, B) as b:
                link = steps(dve, dve_step, b)

                def half_stats(src, h):
                    for k in range(CT):
                        last = dve.bn_stats(bn[:, k, h, :], src[:, k, h * HALF:(h + 1) * HALF])
                    return last

                def group_norm(n, src):
                    for k in range(CT):
                        last = dve.bn_aggr(mv[:, k, :], bn[:, k, :, :])
                    link(last)
                    link(dve.tensor_tensor(g_tmp[:, :], mv[:, :, 0], mv[:, :, 0], ALU.mult))
                    dve.tensor_tensor(mv[:, :, 1], mv[:, :, 1], g_tmp[:, :], ALU.add).then_inc(gn_stats.sem, 1)
                    dve.wait_ge(gn_psum.sem, gn_psum.after(b, n))
                    link(dve.tensor_copy(gs[:, :, :], PS[:, 6 * HALF:6 * HALF + 2 * CT].rearrange("p (m t) -> p m t", t=2)))
                    link(dve.tensor_tensor(g_tmp[:, :], gs[:, :, 0], gs[:, :, 0], ALU.mult))
                    link(dve.tensor_tensor(g_tmp[:, :], gs[:, :, 1], g_tmp[:, :], ALU.subtract))
                    dve.tensor_scalar(g_tmp[:, :], g_tmp[:, :], GN_EPS, None, ALU.add).then_inc(gn_var.sem, 1)
                    dve.wait_ge(gn_rstd.sem, gn_rstd.after(b, n))
                    for k in range(CT):
                        last = dve.tensor_scalar(XN[:, k, :], src[:, k, :], gs[:, k, 0:1], g_rstd[:, k:k + 1],
                                                 ALU.subtract, ALU.mult)
                    last.then_inc(xn_ready.sem, 1)

                half_stats(XN, 0)
                link(half_stats(XN, 1))
                group_norm(1, XN)

                for m, (rows, bank) in enumerate([(P, 0), (XT, 2)]):
                    dve.wait_ge(xh_psum.sem, xh_psum.after(b, m + 1))
                    src = banks(bank)[0:rows, :].rearrange("p (h w) -> p h w", h=IMG)
                    acc = CONV[0:rows, m, :].rearrange("p (h w) -> p h w", h=IMG)
                    wc = COL["conv_w"]
                    last = dve.tensor_scalar(acc, src, wc[0:rows, 9 * m + 4:9 * m + 5],
                                             COL["conv_b"][0:rows, m:m + 1], ALU.mult, ALU.add)
                    for tap in [0, 1, 2, 3, 5, 6, 7, 8]:
                        link(last)
                        dy, dx = tap // 3 - 1, tap % 3 - 1
                        ys, xs_ = (max(0, -dy), IMG - max(0, dy)), (max(0, -dx), IMG - max(0, dx))
                        dst = acc[:, ys[0]:ys[1], xs_[0]:xs_[1]]
                        last = dve.scalar_tensor_tensor(
                            out=dst, in0=src[:, ys[0] + dy:ys[1] + dy, xs_[0] + dx:xs_[1] + dx],
                            scalar=wc[0:rows, 9 * m + tap:9 * m + tap + 1], in1=dst, op0=ALU.mult, op1=ALU.add)
                    last.then_inc(conv_done.sem, 1)

                dve.wait_ge(bc_hi.sem, bc_hi.after(b, 1))
                link(dve.tensor_tensor(REST[:, 0, :], banks(2), BCP[:, 0, :], ALU.subtract))
                link(dve.tensor_copy(BCP[:, 1, :], REST[:, 0, :]))
                link(dve.tensor_tensor(REST[:, 1, :], REST[:, 0, :], BCP[:, 1, :], ALU.subtract))
                dve.tensor_copy(BCP[:, 2, :], REST[:, 1, :]).then_inc(bc_split.sem, 1)

                def soft_series(s):
                    dve.wait_ge(soft_e.sem, soft_e.after(b, s + 1))
                    dve.tensor_scalar(MASK, SE, SMALL, None, ALU.is_lt)
                    dve.scalar_tensor_tensor(out=SQ3, in0=SE, scalar=-1.5, in1=SE, op0=ALU.add,
                                             op1=ALU.mult).then_inc(soft_q2.sem, 1)

                def soft_series_end(s):
                    dve.wait_ge(soft_q2.sem, soft_q2.after(b, s + 1))
                    dve.scalar_tensor_tensor(out=SQ3, in0=SQ3, scalar=3.0, in1=SE, op0=ALU.add,
                                             op1=ALU.mult).then_inc(soft_q.sem, 1)

                def soft_pick(s):
                    dve.wait_ge(soft_ln.sem, soft_ln.after(b, s + 1))
                    dve.wait_ge(soft_q3.sem, soft_q3.after(b, s + 1))
                    dve.copy_predicated(DELTA[:, s % 2, :], MASK, SQ3).then_inc(soft_log.sem, 1)

                def scan(i):
                    s = i // NST
                    dve.wait_ge(da_ready.sem, da_ready.after(b, i + 1))
                    dve.wait_ge(dbu_ready.sem, dbu_ready.after(b, i + 1))
                    if i >= 2:
                        dve.wait_ge(hc_ready.sem, hc_ready.after(b, i - 1))
                    step = 1 if TILE_ORDER[s] < 3 else -1
                    dve.tensor_tensor_scan(HS[:, i % 2, ::step], DA[:, i % 3, ::step], DBU[:, i % R3, ::step],
                                           0.0, ALU.mult, ALU.add).then_inc(scan_done.sem, 1)

                def times_c(i):
                    dve.wait_ge(scan_done.sem, scan_done.after(b, i + 1))
                    dve.wait_ge(cslot_full.sem, cslot_full.after(b, i + 1))
                    if i >= R3:
                        dve.wait_ge(acc_done.sem, acc_done.after(b, i - R3 + 1))
                    dve.tensor_tensor(HC[:, i % R3, :], HS[:, i % 2, :], banks(2 + 2 * (i % 2)), ALU.mult
                                      ).then_inc(hc_ready.sem, 1)

                soft_series(0)
                soft_series_end(0)
                soft_pick(0)
                for i in range(ITEMS):
                    s, n = divmod(i, NST)
                    scan(i)
                    if i:
                        times_c(i - 1)
                    if s < SEQ - 1 and n == 8:
                        soft_series(s + 1)
                    if s < SEQ - 1 and n == 9:
                        soft_series_end(s + 1)
                    if s < SEQ - 1 and n == 10:
                        soft_pick(s + 1)
                times_c(ITEMS - 1)

                def half(h):
                    return slice(h * HALF, (h + 1) * HALF)

                def bank(k, h):
                    return banks(2 * k + h, 1)

                for h in range(2):
                    dve.wait_ge(y_psum.sem, y_psum.after(b, h + 1))
                    for m, rows in ((0, P), (1, XT)):
                        last = dve.scalar_tensor_tensor(out=YF[0:rows, m, half(h)], in0=U[0:rows, m, half(h)],
                                                        scalar=skip_sum[0:rows, m:m + 1], in1=bank(m, h)[0:rows, :],
                                                        op0=ALU.mult, op1=ALU.add)
                    last.then_inc(yf_ready.sem, 1)
                for h in range(2):
                    dve.wait_ge(yf_ready.sem, yf_ready.after(b, h + 1))
                    dve.wait_ge(mean_psum.sem, mean_psum.after(b, h + 1))
                    for m, rows in ((0, P), (1, XT)):
                        last = dve.tensor_tensor(YF[0:rows, m, half(h)], YF[0:rows, m, half(h)], bank(2, h)[0:rows, :],
                                                 ALU.subtract)
                    last.then_inc(yc_ready.sem, 1)
                for h in range(2):
                    dve.wait_ge(rstd_ready.sem, rstd_ready.after(b, h + 1))
                    for m, rows in ((0, P), (1, XT)):
                        last = dve.tensor_tensor(YF[0:rows, m, half(h)], YF[0:rows, m, half(h)], RSTD[0:rows, half(h)],
                                                 ALU.mult)
                    link(last)
                    for m, rows in ((0, P), (1, XT)):
                        last = dve.tensor_scalar(YF[0:rows, m, half(h)], YF[0:rows, m, half(h)],
                                                 COL["norm_g"][0:rows, m:m + 1], COL["norm_b"][0:rows, m:m + 1],
                                                 ALU.mult, ALU.add)
                    link(last)
                    for m, rows in ((0, P), (1, XT)):
                        last = dve.tensor_tensor(YF[0:rows, m, half(h)], YF[0:rows, m, half(h)], ZS[0:rows, m, half(h)],
                                                 ALU.mult)
                    last.then_inc(yg_ready.sem, 1)
                dve.wait_ge(x_loaded.sem, x_loaded.after(b, 1))
                for h in range(2):
                    dve.wait_ge(op_psum.sem, op_psum.after(b, h + 1))
                    for m in range(CT):
                        last = dve.tensor_tensor(X[:, m, half(h)], X[:, m, half(h)], bank(m, h), ALU.add)
                    link(last)
                    last = half_stats(X, h)
                link(last)

                group_norm(2, X)

                def job(g, m):
                    kind, n = JOBS[m]
                    part, h = divmod(n, 2)
                    if kind == "turn":
                        dve.wait_ge(turn_psum.sem, turn_psum.after(b, 4 * g + n + 1))
                        if g or n >= 2:
                            dve.wait_ge(rope_ready.sem, rope_ready.after(b, 4 * g + n - 1))
                        dve.tensor_tensor(RT2[:, h, :], banks(7, 1), W["sin"][:, 0, half(h)], ALU.mult
                                          ).then_inc(sin_done.sem, 1)
                    elif kind == "rel":
                        dve.wait_ge(rel_psum.sem, rel_psum.after(b, 4 * g + n + 1))
                        if g:
                            for loaded in head_loaded:
                                dve.wait_ge(loaded.sem, loaded.after(b, 4 * g))
                        if part == 0:
                            ins = dve.tensor_copy(RELC[:, 0, half(h)], banks(7, 1))
                        else:
                            ins = dve.tensor_copy(
                                RELC[:, 1, :].rearrange("p (h w) -> p w h", h=IMG)[:, h * (IMG // 2):(h + 1) * (IMG // 2), :],
                                banks(7, 1).rearrange("p (w h) -> p w h", h=IMG))
                        ins.then_inc(rel_saved.sem, 1)

                def save_turned(s):
                    n = s // HG
                    dve.wait_ge(pt_psum.sem, pt_psum.after(b, s + 1))
                    if n >= 2:
                        dve.wait_ge(o_psum.sem, o_psum.after(b, n - 1))
                    dve.tensor_copy(PT[:, n % 2, s % HG, :, :], banks(4).rearrange("p (t q) -> p t q", t=QB)
                                    ).then_inc(pt_saved.sem, 1)

                for m in range(len(JOBS)):
                    job(0, m)
                for s in range(STEPS * GROUPS):
                    g, k = divmod(s, STEPS)
                    dve.wait_ge(s_psum.sem, s_psum.after(b, s + 1))
                    if s >= 4:
                        dve.wait_ge(exp_done.sem, exp_done.after(b, s - 3))
                    dve.tensor_reduce(neg_max[:, s % 4:s % 4 + 1], banks(2 * (s % 2)), AX_X, ALU.max,
                                      negate=True).then_inc(max_done.sem, 1)
                    if g + 1 < GROUPS and k - 1 in JOB_AT:
                        job(g + 1, JOB_AT[k - 1])
                    if s % 2 == 1:
                        save_turned(s - 1)

                dve.wait_ge(exp_done.sem, exp_done.after(b, STEPS * GROUPS))
                dve.reciprocal(row_sum[:, :, :], row_sum[:, :, :]).then_inc(rs_ready.sem, 1)
                dve.wait_ge(rb_psum.sem, rb_psum.after(b, 1))
                dve.wait_ge(o_saved.sem, o_saved.after(b, QB * GROUPS))
                for g in range(GROUPS):
                    last = dve.tensor_tensor(OT[:, g, :], OT[:, g, :], banks(2 + 2 * g), ALU.mult)
                link(last)
                for g in range(GROUPS):
                    last = dve.tensor_scalar(OT[:, g, :], OT[:, g, :], COL["b_qkv"][:, 6 + g:7 + g], None, ALU.add)
                last.then_inc(on_ready.sem, 1)
                dve.wait_ge(pj_psum.sem, pj_psum.after(b, 1))
                for m in range(CT):
                    last = dve.scalar_tensor_tensor(out=OUT[:, m, :], in0=banks(2 * m), scalar=COL["b_proj"][:, m:m + 1],
                                                    in1=X[:, m, :], op0=ALU.add, op1=ALU.add)
                last.then_inc(out_ready.sem, 1)
                leave_image(dve, b)

        @block.scalar
        def _(act):
            act.wait_ge(consts.sem, 16 * N_CONST)
            act.wait_ge(prep.sem, 1)
            act.activation(a_neg[:, :], a_low[:, :], ACT.Exp).then_inc(a_exp, 1)
            act.wait_ge(a_exp, 1)
            act.mul(a_neg[:, :], a_neg[:, :], -1.0).then_inc(prep.sem, 1)
            act.wait_ge(prep.sem, 4)

            with act.Fori(0, B) as b:
                link = steps(act, act_step, b)
                act.preload_act_table_set("natural_log_exp_and_others")

                def group_rstd(n):
                    act.wait_ge(gn_var.sem, gn_var.after(b, n))
                    link(act.activation(g_rstd[:, :], g_tmp[:, :], ACT.Ln))
                    act.activation(g_rstd[:, :], g_rstd[:, :], ACT.Exp, scale=-0.5).then_inc(gn_rstd.sem, 1)

                group_rstd(1)
                act.wait_ge(conv_done.sem, conv_done.after(b, 2))

                def by_column(ap):
                    return ap.rearrange("p (h w) -> p w h", h=IMG)

                def grid(ap):
                    return ap.rearrange("p (w h) -> p w h", h=IMG)

                act.activation(U[:, 0, :], CONV[:, 0, :], ACT.Silu)
                act.activation(U[0:XT, 1, :], CONV[0:XT, 1, :], ACT.Silu)
                act.activation(grid(U[XT:P, 1, :]), by_column(CONV[0:XT, 0, :]), ACT.Silu)
                act.activation(grid(U[0:XT, 2, :]), by_column(CONV[XT:P, 0, :]), ACT.Silu)
                act.activation(grid(U[XT:P, 2, :]), by_column(CONV[0:XT, 1, :]), ACT.Silu).then_inc(u_ready.sem, 1)
                act.wait_ge(z_psum.sem, z_psum.after(b, 1))
                act.activation(ZS[:, 0, :], banks(4), ACT.Silu)
                link(act.activation(ZS[0:XT, 1, :], banks(6)[0:XT, :], ACT.Silu))
                act.wait_ge(xdbl_psum.sem, xdbl_psum.after(b, 1))
                act.activation(BCP[:, 0, :], banks(2), ACT.Copy).then_inc(bc_hi.sem, 1)
                act.activation(DTS, banks(0), ACT.Copy).then_inc(dts_saved.sem, 1)

                slot = [0]

                def soft(s):
                    t = TILE_ORDER[s]
                    slot[0] += 1
                    act.wait_ge(bslot_full.sem, bslot_full.after(b, slot[0]))
                    bias = COL["dt_b"][:, t:t + 1]
                    if s:
                        act.wait_ge(delta_ready.sem, delta_ready.after(b, s))
                    link(act.activation(SE, banks(0), ACT.Abs, bias=bias))
                    act.activation(SR, banks(0), ACT.Relu, bias=bias).then_inc(bslot_free.sem, 1)
                    act.activation(SE, SE, ACT.Exp, scale=-1.0).then_inc(soft_e.sem, 1)

                def soft_log1p(s):
                    act.wait_ge(soft_e.sem, soft_e.after(b, s + 1))
                    act.activation(DELTA[:, s % 2, :], SE, ACT.Ln, bias=one[:, 0:1]).then_inc(soft_ln.sem, 1)

                def soft_third(s):
                    act.wait_ge(soft_q.sem, soft_q.after(b, s + 1))
                    act.activation(SQ3, SQ3, ACT.Copy, scale=1.0 / 3.0).then_inc(soft_q3.sem, 1)

                def decay(i):
                    s, n = divmod(i, NST)
                    if n == 0:
                        act.wait_ge(delta_ready.sem, delta_ready.after(b, s + 1))
                    if i >= 3:
                        act.wait_ge(scan_done.sem, scan_done.after(b, i - 2))
                    at = TILE_ORDER[s] * NST + n
                    act.activation(DA[:, i % 3, :], DELTA[:, s % 2, :], ACT.Exp, bias=a_inf[:, at:at + 1],
                                   scale=a_neg[:, at:at + 1]).then_inc(da_ready.sem, 1)

                act.preload_act_table_set("natural_log_exp_and_others")
                soft(0)
                soft_log1p(0)
                soft_third(0)
                for i in range(ITEMS):
                    s, n = divmod(i, NST)
                    slot[0] += 1
                    act.wait_ge(bslot_full.sem, bslot_full.after(b, slot[0]))
                    if i >= R3:
                        act.wait_ge(dbu_ready.sem, dbu_ready.after(b, i - R3 + 1))
                    act.activation(BSB[:, i % R3, :], banks(0), ACT.Copy).then_inc(bslot_free.sem, 1)
                    decay(i)
                    if n == DT_AT and s < SEQ - 1:
                        soft(s + 1)
                    if n == 10 and s < SEQ - 1:
                        soft_log1p(s + 1)
                    if n == 12 and s < SEQ - 1:
                        soft_third(s + 1)
                    pair, k = divmod(i, 2 * NST)
                    if (k == ACC_LAG - 1 and pair) or i == ITEMS - 1:
                        done = pair if i != ITEMS - 1 else pair + 1
                        act.wait_ge(acc_done.sem, acc_done.after(b, 2 * NST * done))
                        act.activation(YSB[:, done - 1, :], banks(6), ACT.Copy).then_inc(y_saved.sem, 1)

                def half(h):
                    return slice(h * HALF, (h + 1) * HALF)

                for h in range(2):
                    act.wait_ge(yc_ready.sem, yc_ready.after(b, h + 1))
                    act.activation(SQ[:, 0, half(h)], YF[:, 0, half(h)], ACT.Square)
                    act.activation(SQ[0:XT, 1, half(h)], YF[0:XT, 1, half(h)], ACT.Square).then_inc(sq_ready.sem, 1)
                for h in range(2):
                    act.wait_ge(var_psum.sem, var_psum.after(b, h + 1))
                    link(act.activation(RSTD[:, half(h)], banks(6 + h, 1), ACT.Ln, bias=eps[:, 0:1]))
                    act.activation(RSTD[:, half(h)], RSTD[:, half(h)], ACT.Exp, scale=-0.5).then_inc(rstd_ready.sem, 1)

                group_rstd(2)

                def save_v(t):
                    act.wait_ge(v_psum.sem, v_psum.after(b, t + 1))
                    act.activation(V[:, t, :], banks(t % 4, 1)[:, 0:C], ACT.Copy).then_inc(v_saved.sem, 1)

                def job(g, m):
                    kind, n = JOBS[m]
                    side, h = divmod(n, 2)
                    if kind != "proj":
                        return
                    act.wait_ge(proj_psum.sem, proj_psum.after(b, 4 * g + n + 1))
                    if g or n >= 2:
                        act.wait_ge(turn_psum.sem, turn_psum.after(b, 4 * g + n - 1))
                        act.wait_ge(cos_done.sem, cos_done.after(b, 4 * g + n - 1))
                    bias = COL["b_qkv"][:, g:g + 1] if side == 0 else bk_scaled[:, g:g + 1]
                    act.activation(RAW[:, h, :], banks(7, 1), ACT.Identity, bias=bias,
                                   scale=1.0 if side == 0 else ATT_SCALE).then_inc(raw_saved.sem, 1)

                def save_turned(s):
                    n = s // HG
                    act.wait_ge(pt_psum.sem, pt_psum.after(b, s + 1))
                    if n >= 2:
                        act.wait_ge(o_psum.sem, o_psum.after(b, n - 1))
                    act.activation(PT[:, n % 2, s % HG, :, :], banks(4).rearrange("p (t q) -> p t q", t=QB),
                                   ACT.Copy).then_inc(pt_saved.sem, 1)

                def save_sums(n):
                    g, qb = divmod(n, QB)
                    act.wait_ge(o_psum.sem, o_psum.after(b, n + 1))
                    act.activation(OT[:, g, qb * P:(qb + 1) * P], banks(6, 1)[:, (n % 2) * P:(n % 2 + 1) * P],
                                   ACT.Copy).then_inc(o_saved.sem, 1)

                for m in range(len(JOBS)):
                    job(0, m)
                    if m < QB:
                        save_v(m)
                for s in range(STEPS * GROUPS):
                    g, k = divmod(s, STEPS)
                    qb, j = divmod(k, HG)
                    act.wait_ge(max_done.sem, max_done.after(b, s + 1))
                    if s >= 2:
                        act.wait_ge(pt_psum.sem, pt_psum.after(b, s - 1))
                    at = HG * g + j
                    act.activation(PR[:, s % 2, :], banks(2 * (s % 2)), ACT.Exp, bias=neg_max[:, s % 4:s % 4 + 1],
                                   accum_out=row_sum[:, qb, at:at + 1]).then_inc(exp_done.sem, 1)
                    if g + 1 < GROUPS and k - 1 in JOB_AT:
                        job(g + 1, JOB_AT[k - 1])
                    if s and s % 2 == 0:
                        save_turned(s - 1)
                    if s % HG == 3 and s > HG:
                        save_sums(s // HG - 1)
                save_turned(STEPS * GROUPS - 1)
                save_sums(QB * GROUPS - 1)
                act.wait_ge(rt_psum.sem, rt_psum.after(b, 1))
                act.activation(RT[0:NH, :], banks(0)[0:NH, :], ACT.Copy).then_inc(rt_saved.sem, 1)
                leave_image(act, b)

        @block.gpsimd
        def _(pool):
            with pool.Fori(0, B) as b:
                def delta(s):
                    pool.wait_ge(soft_log.sem, soft_log.after(b, s + 1))
                    pool.tensor_tensor(DELTA[:, s % 2, :], DELTA[:, s % 2, :], SR, ALU.add
                                       ).then_inc(delta_ready.sem, 1)

                def times_u(s):
                    pool.wait_ge(delta_ready.sem, delta_ready.after(b, s + 1))
                    pool.tensor_tensor(DU[:, s % 2, :], DELTA[:, s % 2, :], U[:, TILE_ORDER[s] % 3, :], ALU.mult
                                       ).then_inc(du_ready.sem, 1)

                delta(0)
                times_u(0)
                for i in range(ITEMS):
                    s, n = divmod(i, NST)
                    if n == 0:
                        pool.wait_ge(du_ready.sem, du_ready.after(b, s + 1))
                    pool.wait_ge(bslot_free.sem, bslot_free.after(b, i + 1 + dt_before(i)))
                    if i >= R3:
                        pool.wait_ge(scan_done.sem, scan_done.after(b, i - R3 + 1))
                    pool.tensor_tensor(DBU[:, i % R3, :], DU[:, s % 2, :], BSB[:, i % R3, :], ALU.mult
                                       ).then_inc(dbu_ready.sem, 1)
                    if s < SEQ - 1 and n == 12:
                        delta(s + 1)
                    if s < SEQ - 1 and n == 14:
                        times_u(s + 1)
                for g in range(GROUPS):
                    for n in range(4):
                        side, h = divmod(n, 2)
                        at = slice(h * HALF, (h + 1) * HALF)
                        if g == 0 and n == 0:
                            pool.wait_ge(att_loaded.sem, att_loaded.after(b, len(ATT_MATS)))
                        pool.wait_ge(raw_saved.sem, raw_saved.after(b, 4 * g + n + 1))
                        pool.tensor_tensor(RT1[:, h, :], RAW[:, h, :], W["cos"][:, 0, at], ALU.mult
                                           ).then_inc(cos_done.sem, 1)
                        pool.wait_ge(cos_done.sem, cos_done.after(b, 4 * g + n + 1))
                        pool.wait_ge(sin_done.sem, sin_done.after(b, 4 * g + n + 1))
                        if g and n == 0:
                            for loaded in head_loaded:
                                pool.wait_ge(loaded.sem, loaded.after(b, 4 * g))
                        pool.tensor_tensor(QKC[:, side, at], RT1[:, h, :], RT2[:, h, :], ALU.add
                                           ).then_inc(rope_ready.sem, 1)
                leave_image(pool, b)


def dt_before(i):
    s, n = divmod(i, NST)
    return 1 + s + (1 if n > DT_AT and s < SEQ - 1 else 0)


def kernel(x, L0_conv_in_proj_w, L0_conv_conv_w, L0_conv_conv_b, L0_conv_x_proj_w, L0_conv_dt_projs_w,
           L0_conv_dt_projs_b, L0_conv_A_logs, L0_conv_Ds, L0_conv_out_norm_g, L0_conv_out_norm_b,
           L0_conv_out_proj_w, L1_conv_w_qkv, L1_conv_b_qkv, L1_conv_w_proj, L1_conv_b_proj,
           L1_conv_rel_pos_h, L1_conv_rel_pos_w):
    import ml_dtypes
    import numpy as np
    import concourse.bacc as bacc
    from concourse.bass_utils import run_bass_kernel_spmd

    f = np.float32

    def halves(v):
        v = np.asarray(v)
        o = np.zeros((P, 2) + v.shape[1:], f)
        o[:, 0] = v[:P]
        o[:XT, 1] = v[P:]
        return o

    def tiles(v):
        return np.ascontiguousarray(np.asarray(v).reshape(-1, P).T)

    mats, cols = {}, {}
    mats["w_in"] = np.asarray(L0_conv_in_proj_w).T
    xp = np.asarray(L0_conv_x_proj_w)
    w = np.zeros((2, DI, 2 * P), f)
    for k in range(DIRS):
        order = k % 2
        w[order, :, 32 * k:32 * k + RANK] = xp[k, :RANK].T
        for c in range(2):
            at = P + 64 * (k // 2) + 32 * c + NST * (k % 2)
            w[order, :, at:at + NST] = xp[k, RANK + NST * c:RANK + NST * (c + 1)].T
    mats["w_xdbl"] = np.concatenate([w[0], w[1]])
    wd = np.zeros((P, DIRS * DI), f)
    for k in range(DIRS):
        wd[32 * k:32 * k + RANK, DI * k:DI * (k + 1)] = np.asarray(L0_conv_dt_projs_w)[k].T
    mats["w_dt"] = wd
    wo = np.zeros((2 * P, C), f)
    wo[:DI] = np.asarray(L0_conv_out_proj_w).T
    mats["w_out"] = wo
    mats["w_qkv"] = np.asarray(L1_conv_w_qkv)
    mats["w_proj"] = np.asarray(L1_conv_w_proj)
    ch = np.arange(C)
    mats["group_mean"] = (ch[:, None] // 12 == ch[None, :] // 12) / f(12)
    freqs = (1.0 / np.power(f(10000.0), np.arange(0, HD, 4, dtype=f) / f(HD))).astype(f)
    tok = np.arange(L)
    ang = np.concatenate([(tok % IMG).astype(f)[:, None] * freqs, (tok // IMG).astype(f)[:, None] * freqs], 1)
    rows = (np.arange(P) % HD) // 2
    mats["cos"] = np.cos(ang).T[rows]
    mats["sin"] = np.sin(ang).T[rows]
    mats["ident"] = np.eye(P)
    mats["to_low"] = np.eye(P, k=-XT)
    mats["to_high"] = np.eye(P, k=XT)
    turn = np.zeros((P, P), f)
    for i in range(0, P, 2):
        turn[i + 1, i] = -1.0
        turn[i, i + 1] = 1.0
    mats["turn"] = turn
    mats["chan_mean"] = np.full((P, P), 1.0 / DI)
    hr = np.zeros((NH, C), f)
    hr[ch // HD, ch] = 1.0
    mats["head_rows"] = hr
    for name, table in (("rel_h", L1_conv_rel_pos_h), ("rel_w", L1_conv_rel_pos_w)):
        rel = np.zeros((HG, HD, REL, HG), f)
        for j in range(HG):
            rel[j, :, :, j] = np.asarray(table)[:REL][::-1].T
        mats[name] = rel.reshape(P, HG * REL)

    cols["conv_w"] = halves(np.asarray(L0_conv_conv_w).reshape(DI, 9)).reshape(P, 18)
    cols["conv_b"] = halves(L0_conv_conv_b)
    cols["dt_b"] = tiles(np.asarray(L0_conv_dt_projs_b).reshape(-1))
    cols["a_log"] = np.asarray(L0_conv_A_logs).reshape(SEQ, P, NST).transpose(1, 0, 2).reshape(P, SEQ * NST)
    cols["skip"] = halves(np.asarray(L0_conv_Ds).reshape(DIRS, DI).T).reshape(P, 2 * DIRS)
    cols["norm_g"] = halves(L0_conv_out_norm_g)
    cols["norm_b"] = halves(L0_conv_out_norm_b)
    cols["b_qkv"] = tiles(L1_conv_b_qkv)
    cols["b_proj"] = tiles(L1_conv_b_proj)

    sel = np.zeros((3, 2, NST, 3, NST, P), f)
    for n in range(NST):
        sel[:, 0, n, 0, n, :] = 1
        sel[:, 0, n, 1, n, :XT] = 1
        sel[:, 1, n, 1, n, XT:] = 1
        sel[:, 1, n, 2, n, :] = 1
    sel = sel.reshape(3 * 2 * NST, 3 * NST, P).astype(ml_dtypes.bfloat16)
    onehot = np.zeros((2 * IMG, L), f)
    onehot[tok // IMG, tok] = 1
    onehot[IMG + tok % IMG, tok] = 1
    xt = np.ascontiguousarray(np.asarray(x).reshape(B, L, C).transpose(0, 2, 1))

    nc = bacc.Bacc("TRN2", target_bir_lowering=False, num_devices=1)
    arrays = {}

    def given(name, a, dtype=f):
        a = np.ascontiguousarray(a, dtype)
        arrays[name] = a
        return nc.dram_tensor(name, a.shape, mybir.dt.from_np(a.dtype), kind="ExternalInput").ap()

    x_ap = given("x_in", xt)
    mat_aps = {k: given(k + "_in", v) for k, v in mats.items()}
    col_aps = {k: given(k + "_in", v) for k, v in cols.items()}
    sel_ap = given("sel_in", sel, ml_dtypes.bfloat16)
    onehot_ap = given("onehot_in", onehot)
    out_ap = nc.dram_tensor("out_t", (B, C, L), F32, kind="ExternalOutput").ap()
    build(nc, x_ap, mat_aps, col_aps, sel_ap, onehot_ap, out_ap)
    r = run_bass_kernel_spmd(nc, [arrays], core_ids=[0])
    got = np.asarray(r.results[0]["out_t"])
    return np.ascontiguousarray(got.transpose(0, 2, 1)).reshape(B, IMG, IMG, C)
```

```python
from contextlib import ExitStack

import concourse.bass as bass
from concourse import mybir

P = 128
B, IMG, C = 4, 32, 384
L = IMG * IMG
CT = C // P
HALF = L // 2
DI, NST, RANK, DIRS = 192, 16, 24, 4
SEQ = DIRS * DI // P
XT = 64
ITEMS = SEQ * NST
NH, HD = 12, 32
HG = P // HD
GROUPS = NH // HG
QB = L // P
STEPS = QB * HG
REL = 2 * IMG - 1
ATT_SCALE = float(HD) ** -0.5
GN_EPS = 1e-5
LN_EPS = 1e-5
SMALL = 2.0 ** -7
DT_AT, EXP_AT, LN_AT, SERIES_AT, SERIES_END_AT, THIRD_AT, PICK_AT, DELTA_AT, DU_AT = 6, 7, 9, 7, 8, 11, 9, 11, 13
C_LAG, ACC_LAG = 3, 5
A_LOG_MAX = 80.0
TILE_ORDER = [0, 3, 1, 4, 2, 5]

F32 = mybir.dt.float32
BF16 = mybir.dt.bfloat16
U8 = mybir.dt.uint8
ALU = mybir.AluOpType
ACT = mybir.ActivationFunctionType
AX_X = mybir.AxisListType.X

KEPT = {
    "group_mean": (3 * P, C), "ident": (P, P), "to_low": (P, P), "to_high": (P, P), "turn": (P, P),
    "chan_mean": (P, P), "head_rows": (NH, C), "rel_h": (P, REL * HG), "rel_w": (P, REL * HG),
}
SCAN_MATS = {"w_in": (3 * P, C), "w_xdbl": (3 * P, 2 * P), "w_dt": (P, SEQ * P)}
ATT_MATS = {"w_qkv": (3 * P, 3 * C), "cos": (P, L), "sin": (P, L)}
TAIL_MATS = {"w_out": (2 * P, C), "w_proj": (3 * P, C)}
COLS = {
    "conv_w": 2 * 9, "conv_b": 2, "dt_b": SEQ, "a_log": SEQ * NST, "skip": 2 * DIRS,
    "norm_g": 2, "norm_b": 2, "b_qkv": 9, "b_proj": 3,
}


class Signal:

    def __init__(self, sem, per_image, unit=1):
        self.sem, self.per_image, self.unit = sem, per_image, unit

    def after(self, b, n):
        return n * self.unit


def build(nc, x, mats, cols, sel_in, onehot, out):
    ctx = ExitStack()
    with ctx:
        def sb(name, shape, dt=F32):
            return ctx.enter_context(nc.sbuf_tensor(name, shape, dt))

        def signal(name, per_image, unit=1):
            return Signal(ctx.enter_context(nc.semaphore(name)), per_image, unit)

        X = sb("residual", [P, CT, L])
        XN = sb("normed", [P, CT, L])
        W = {}
        for name, (rows, width) in (KEPT | TAIL_MATS).items():
            W[name] = sb(name, [min(rows, P), max(rows // P, 1), width])
        COL = {name: sb(name, [P, width]) for name, width in COLS.items()}
        one = sb("one", [P, 1])
        eps = sb("eps", [P, 1])
        a_neg = sb("a_neg", [P, SEQ * NST])
        a_low = sb("a_low", [P, SEQ * NST])
        a_inf = sb("a_inf", [P, SEQ * NST])
        skip_sum = sb("skip_sum", [P, 2])
        bk_scaled = sb("bk_scaled", [P, GROUPS])
        bn = sb("bn", [P, CT, 2, 6])
        mv = sb("mv", [P, CT, 2])
        gs = sb("gs", [P, CT, 2])
        g_tmp = sb("g_tmp", [P, CT])
        g_rstd = sb("g_rstd", [P, CT])
        neg_max = sb("neg_max", [P, 4])
        row_sum = sb("row_sum", [P, QB, NH])
        M0 = -(-max(sum(max(rows // P, 1) * width for rows, width in ATT_MATS.values()),
                    sum(max(rows // P, 1) * width for rows, width in SCAN_MATS.values()) + 3 * NST * P // 2) // HALF)
        arena = sb("arena", [P, M0 * HALF + 34 * L])
        PS = ctx.enter_context(nc.psum_tensor("PS", [P, 8 * HALF], F32))

        def banks(k, n=2):
            return PS[:, k * HALF:(k + n) * HALF]

        PADDED = PS[:, 2 * HALF:2 * HALF + (IMG // 2 + 2) * IMG]

        def place_mats(which, at):
            for name, (rows, width) in which.items():
                k = max(rows // P, 1)
                W[name] = arena[:, at:at + k * width].rearrange("p (k c) -> p k c", k=k)
                at += k * width
            return at

        at = place_mats(SCAN_MATS, 0)
        SEL = arena[0:3 * 2 * NST, at:at + 3 * NST * P // 2].bitcast(BF16).rearrange("p (s c) -> p s c", c=P)
        place_mats(ATT_MATS, 0)

        def from_mats(k, n=1):
            o = M0 * HALF + k * L
            return arena[:, o:o + n * L].rearrange("p (n l) -> p n l", n=n)

        U, YSB, ZS, DTS = from_mats(0, 3), from_mats(3, 3), from_mats(6, 2), from_mats(8)[:, 0, :]
        BCS = from_mats(9, 2).rearrange("p n l -> p (n l)").bitcast(BF16).rearrange("p (g l) -> p g l", g=4)
        DELTA, DU = from_mats(11, 2), from_mats(13, 2)
        SE, SQ3, SR = [from_mats(15 + k)[:, 0, :] for k in range(3)]
        MASK = from_mats(18)[:, 0, 0:L // 4].bitcast(U8)
        R3, R_HC = 3, 4
        HS, DA, BSB, DBU, HC = (from_mats(19, 2), from_mats(21, 3), from_mats(24, R3), from_mats(27, R3),
                                from_mats(30, R_HC))
        CONV = from_mats(19, 2)
        BCP = from_mats(21, 2).rearrange("p n l -> p (n l)").bitcast(BF16)[:, 0:3 * L].rearrange(
            "p (a l) -> p a l", a=3)
        REST = from_mats(23, 2)
        YF, SQ, RSTD = from_mats(11, 2), from_mats(13, 2), from_mats(15)[:, 0, :]
        QX, KX = from_mats(19, HG), from_mats(23, HG)
        V = from_mats(0, 3).rearrange("p n l -> p (n l)").rearrange("p (t c) -> p t c", t=QB)
        OT = from_mats(3, 3)
        PR = from_mats(6, 2)
        QKC = from_mats(8, 3)
        RELC = from_mats(30, 4).rearrange("p (g a) l -> p g a l", g=2)
        PT = from_mats(11, 8).rearrange("p n l -> p (n l)").rearrange("p (s j t q) -> p s j t q", s=2, j=HG, t=QB)
        RAW = [from_mats(k)[:, 0, h * HALF:(h + 1) * HALF] for k in (27, 17) for h in range(2)]
        RT1, RT2 = [from_mats(28 + k)[:, 0, :].rearrange("p (s l) -> p s l", s=2) for k in range(2)]
        OUT = from_mats(27, 3)
        RT = from_mats(10)[:, 0, :]

        columns = signal("columns_loaded", 0, 16)
        consts = signal("consts_loaded", 0, 16)
        prep = signal("consts_prepared", 0)
        a_exp = ctx.enter_context(nc.semaphore("a_exp"))
        image_done = ctx.enter_context(nc.semaphore("image_done"))
        clearing = ctx.enter_context(nc.semaphore("clearing"))
        image_open = ctx.enter_context(nc.semaphore("image_open"))
        first_x = signal("first_x", 0, 16)
        first_mats = signal("first_mats", 0, 16)
        first_gn = [signal(f"first_gn_{k}", 1) for k in ("stats", "psum", "var", "rstd")]
        xn_first = signal("xn_first", 1)
        first_step = signal("first_step", 0)
        out_stored = ctx.enter_context(nc.semaphore("out_stored"))
        conv_input_done = ctx.enter_context(nc.semaphore("conv_input_done"))
        x_loaded = signal("x_loaded", 1, 16)
        next_loaded = signal("next_loaded", 5, 16)
        att_loaded = signal("att_loaded", len(ATT_MATS), 16)
        gn_stats = signal("gn_stats", 2)
        gn_psum = signal("gn_psum", 2)
        gn_var = signal("gn_var", 2)
        gn_rstd = signal("gn_rstd", 2)
        xn_ready = signal("xn_ready", 3)
        xh_psum = signal("xh_psum", 1)
        pads_zero = signal("pads_zero", 1)
        z_psum = signal("z_psum", 1)
        centre_done = signal("centre_done", 2)
        conv_done = signal("conv_done", 2)
        u_ready = signal("u_ready", 2)
        z_read = signal("z_read", 1)
        xdbl_psum = signal("xdbl_psum", 2)
        dts_saved = signal("dts_saved", 1)
        bc_hi = signal("bc_hi", 1)
        bc_mid = signal("bc_mid", 1)
        bc_split = signal("bc_split", 1)
        bcs_loaded = signal("bcs_loaded", 12, 16)
        bslot_full = signal("bslot_full", ITEMS + SEQ)
        bslot_free = signal("bslot_free", ITEMS + SEQ)
        cslot_full = signal("cslot_full", ITEMS)
        soft_e = signal("soft_e", SEQ)
        soft_ln = signal("soft_ln", SEQ)
        soft_q = signal("soft_q", SEQ)
        soft_q2 = signal("soft_q2", SEQ)
        soft_q3 = signal("soft_q3", SEQ)
        soft_log = signal("soft_log", SEQ)
        delta_ready = signal("delta_ready", SEQ)
        du_ready = signal("du_ready", SEQ)
        da_ready = signal("da_ready", ITEMS)
        dbu_ready = signal("dbu_ready", ITEMS)
        scan_done = signal("scan_done", ITEMS)
        hc_ready = signal("hc_ready", ITEMS)
        acc_done = signal("acc_done", ITEMS)
        y_saved = signal("y_saved", 3)
        y_psum = signal("y_psum", 2)
        yf_ready = signal("yf_ready", 2)
        mean_psum = signal("mean_psum", 2)
        yc_ready = signal("yc_ready", 2)
        sq_ready = signal("sq_ready", 2)
        var_psum = signal("var_psum", 2)
        rstd_ready = signal("rstd_ready", 2)
        yg_ready = signal("yg_ready", 2)
        op_psum = signal("op_psum", 2 * CT)
        x_added = signal("x_added", 2 * CT)
        v_psum = signal("v_psum", QB)
        v_saved = signal("v_saved", QB)
        onehot_loaded = signal("onehot_loaded", HG, 16)
        proj_psum = signal("proj_psum", 4 * GROUPS)
        raw_saved = signal("raw_saved", 4 * GROUPS)
        cos_done = signal("cos_done", 4 * GROUPS)
        turn_psum = signal("turn_psum", 4 * GROUPS)
        sin_done = signal("sin_done", 4 * GROUPS)
        rope_ready = signal("rope_ready", 4 * GROUPS)
        rel_psum = signal("rel_psum", 12)
        rel_saved = signal("rel_saved", 12)
        head_loaded = [signal(f"head{j}_loaded", 4 * GROUPS, 16) for j in range(HG)]
        s_psum = signal("s_psum", STEPS * GROUPS)
        max_done = signal("max_done", STEPS * GROUPS)
        exp_done = signal("exp_done", STEPS * GROUPS)
        pt_psum = signal("pt_psum", STEPS * GROUPS)
        pt_saved = signal("pt_saved", STEPS * GROUPS)
        o_psum = signal("o_psum", QB * GROUPS)
        o_saved = signal("o_saved", QB * GROUPS)
        rs_ready = signal("rs_ready", 3)
        rt_psum = signal("rt_psum", 4)
        rt_saved = signal("rt_saved", 4)
        rb_psum = signal("rb_psum", 2 * GROUPS)
        on_ready = signal("on_ready", 2 * GROUPS)
        pj_psum = signal("pj_psum", 2 * CT)
        pj_read = signal("pj_read", 2 * CT)
        dve_step = signal("dve_step", 0)
        act_step = signal("act_step", 0)

        def steps(eng, sig, b):
            count = [0]

            def link(ins):
                count[0] += 1
                ins.then_inc(sig.sem, 1)
                eng.wait_ge(sig.sem, sig.after(b, count[0]))
            return link

        per_image = range(x_loaded.sem.num, act_step.sem.num + 1)

        def leave_image(eng, b):
            eng.sem_inc(image_done, 1)
            eng.wait_ge(image_open, b + 1)


        PREPARED = [(0, "q"), (0, "k"), (1, "q"), (2, "q"), (1, "k"), (2, "k")]
        PLACE = {(0, "q"): 0, (0, "k"): 1, (1, "q"): 0, (2, "q"): 2, (1, "k"): 1, (2, "k"): 1}
        JOBS = [[(kind, n) for kind in ("proj", "turn", "rel") for n in range(4)],
                [("proj", 4), ("proj", 5), ("turn", 4), ("turn", 5), ("proj", 6), ("proj", 7), ("turn", 6),
                 ("turn", 7), ("proj", 8), ("proj", 9)] + [("rel", n) for n in range(4, 12)]
                + [("turn", 8), ("turn", 9)],
                [("proj", 10), ("proj", 11), ("turn", 10), ("turn", 11)]]
        START = [(m, ()) for m in range(5)] + [(5, (0,)), (6, ()), (7, (1,)), (8, (2,)), (9, (3,)), (10, (4,)),
                                               (11, (5,)), (None, (6, 7))]
        JOB_AT = [{2 + m * 7 // 5: m for m in range(len(JOBS[1]))}, {6 + 4 * m: m for m in range(len(JOBS[2]))}, {}]
        ROPE_FOR, REL_FOR = [4, 10, 12], [4, 12, 12]

        def job_bank(phase, m):
            return 7 if phase else 4 + m % 4

        def last_use(n):
            return n - 4 if n < 6 else n - 2

        LATE = [("sums", 0), ("norm", 0, 0), ("norm", 1, 0), ("sums", 1), ("norm", 0, 1), ("norm", 1, 1),
                ("next",), None, None, ("sums", 2), ("norm", 2, 0), ("proj", 0, 0), ("proj", 1, 0), ("proj", 2, 0)]
        LATE_AT = {2 * m + 2: job for m, job in enumerate(LATE) if job}

        def norm_count(g, h):
            return 2 * h + g + 1 if g < 2 else 5 + h

        N_COLUMNS = len(COLS) + 1
        LATER = [name for name in KEPT if name != "group_mean"]
        N_CONST = len(LATER) + len(TAIL_MATS)
        block = ctx.enter_context(nc.Block())

        @block.sync
        def _(sp):
            def load_mats(which, sig):
                for name in which:
                    rows = which[name][0]
                    at = W[name][:, :, :] if name in KEPT or name in TAIL_MATS else W[name]
                    sp.dma_start(at, mats[name].rearrange("(k p) c -> p k c", k=max(rows // P, 1))
                                 ).then_inc(sig.sem, 16)

            def load_scan(i, sig):
                sp.dma_start(XN[:, :, :], x[bass.ds(i, 1), :, :].rearrange("o (k p) l -> p (o k) l", p=P)
                             ).then_inc(sig.sem, 16)
                load_mats(SCAN_MATS, sig)
                sp.dma_start(SEL, sel_in).then_inc(sig.sem, 16)

            sp.sem_inc(out_stored, 2 * 16)
            sp.dma_start(XN[:, :, :], x[0:1, :, :].rearrange("o (k p) l -> p (o k) l", p=P)).then_inc(first_x.sem, 16)
            for name in COLS:
                sp.dma_start(COL[name][:, :], cols[name]).then_inc(columns.sem, 16)
            load_mats({"group_mean": KEPT["group_mean"]}, columns)
            load_mats(SCAN_MATS, first_mats)
            sp.dma_start(SEL, sel_in).then_inc(first_mats.sem, 16)
            load_mats({name: KEPT[name] for name in LATER}, consts)
            load_mats(TAIL_MATS, consts)
            with sp.Fori(0, B) as b:
                sp.dma_start(X[:, :, :], x[bass.ds(b, 1), :, :].rearrange("o (k p) l -> p (o k) l", p=P)
                             ).then_inc(x_loaded.sem, 16)
                sp.wait_ge(out_stored, 2 * 16 * (b + 1))
                for part, ready in enumerate((bc_hi, bc_mid, bc_split)):
                    sp.wait_ge(ready.sem, ready.after(b, 1))
                    for g in range(4):
                        sp.dma_start(BCS[32 * part:32 * part + 32, g, :], BCP[32 * g:32 * g + 32, part, :]
                                     ).then_inc(bcs_loaded.sem, 16)
                sp.wait_ge(acc_done.sem, acc_done.after(b, ITEMS))
                load_mats(ATT_MATS, att_loaded)
                for j in range(HG):
                    sp.dma_start(KX[HD:3 * HD, j, :], onehot).then_inc(onehot_loaded.sem, 16)

                def operands(g, j):
                    rows = slice(HD * j, HD * j + HD)
                    return [(QX[0:HD, j, :], QKC[rows, PLACE[g, "q"], :]),
                            (KX[0:HD, j, :], QKC[rows, PLACE[g, "k"], :]),
                            (QX[HD:2 * HD, j, :], RELC[j::HG, g // 2, 0, :]),
                            (QX[2 * HD:3 * HD, j, :], RELC[j::HG, g // 2, 1, :])]

                for k, (ready, count) in enumerate(((rope_ready, 2), (rope_ready, 4), (rel_saved, 2), (rel_saved, 4))):
                    sp.wait_ge(ready.sem, ready.after(b, count))
                    for j in range(HG):
                        dst, src = operands(0, j)[k]
                        sp.dma_start(dst, src).then_inc(head_loaded[j].sem, 16)
                for g in range(1, GROUPS):
                    sp.wait_ge(rope_ready.sem, rope_ready.after(b, ROPE_FOR[g]))
                    sp.wait_ge(rel_saved.sem, rel_saved.after(b, REL_FOR[g]))
                    for j in range(HG):
                        sp.wait_ge(s_psum.sem, s_psum.after(b, STEPS * g - HG + j + 1))
                        for dst, src in operands(g, j):
                            sp.dma_start(dst, src).then_inc(head_loaded[j].sem, 16)
                load_scan((b + 1) % B, next_loaded)
                for h in range(2):
                    sp.wait_ge(pj_read.sem, pj_read.after(b, CT * (h + 1)))
                    at = slice(h * HALF, (h + 1) * HALF)
                    sp.dma_start(out[bass.ds(b, 1), :, at].rearrange("o (k p) l -> p (o k) l", p=P), OUT[:, :, at]
                                 ).then_inc(out_stored, 16)
                sp.wait_ge(image_done, 4 * b + 4)
                sp.sem_inc(clearing, 1)
                sp.sem_clear(per_image)
                sp.sem_inc(image_open, 1)
            sp.wait_ge(out_stored, 2 * 16 * (B + 1))

        @block.tensor
        def _(pe):
            pe.wait_ge(columns.sem, 16 * N_COLUMNS)

            def half_product(dst, h, pairs):
                for k, (lhs, rhs) in enumerate(pairs):
                    last = pe.matmul(dst, lhs, rhs(h), start=(k == 0), stop=(k == len(pairs) - 1))
                return last

            def product(dst, pairs):
                for h in range(2):
                    for k, (lhs, rhs) in enumerate(pairs):
                        last = pe.matmul(dst[:, h * HALF:(h + 1) * HALF], lhs, rhs(h),
                                         start=(k == 0), stop=(k == len(pairs) - 1))
                return last

            def flat(ap):
                return lambda h: ap[:, h * HALF:(h + 1) * HALF]

            def turned(ap):
                return lambda h: ap.rearrange("p (w h) -> p h w", h=IMG)[:, h * (IMG // 2):(h + 1) * (IMG // 2), :]

            def group_stats(ready, done, n, bank):
                pe.wait_ge(ready.sem, n)
                for m in range(CT):
                    near = [k for k in range(CT) if abs(k - m) <= 1]
                    for k in near:
                        last = pe.matmul(PS[:, bank * HALF + 2 * m:bank * HALF + 2 * m + 2],
                                         W["group_mean"][:, k, m * P:(m + 1) * P], mv[:, k, :],
                                         start=(k == near[0]), stop=(k == near[-1]), skip_group_check=True)
                last.then_inc(done.sem, 1)

            group_stats(first_gn[0], first_gn[1], 1, 7)
            pe.wait_ge(xn_first.sem, 1)
            pe.wait_ge(first_mats.sem, first_mats.after(0, len(SCAN_MATS) + 1))
            xn = [flat(XN[:, k, :]) for k in range(CT)]

            def conv_input():
                product(banks(4), [(W["w_in"][:, k, 0:P], xn[k]) for k in range(CT)]).then_inc(conv_input_done, 1)

            conv_input()
            with pe.Fori(0, B) as b:
                pe.wait_ge(pads_zero.sem, pads_zero.after(b, 1))
                for part, row, first_row, n_rows in ((0, 1, 0, 15), (0, 16, 15, 2), (1, 0, 15, 16), (1, 16, 31, 1)):
                    for k in range(CT):
                        last = pe.matmul(PADDED[XT * part:XT * part + XT, row * IMG:(row + n_rows) * IMG],
                                         W["w_in"][:, k, P:DI], XN[:, k, first_row * IMG:(first_row + n_rows) * IMG],
                                         start=(k == 0), stop=(k == CT - 1), skip_group_check=True)
                last.then_inc(xh_psum.sem, 1)
                for c0, rows, bank in ((DI, P, 0), (DI + P, XT, 6)):
                    last = product(banks(bank)[0:rows, :],
                                   [(W["w_in"][:, k, c0:c0 + rows], xn[k]) for k in range(CT)])
                last.then_inc(z_psum.sem, 1)
                def x_proj(which, k):
                    for h in range(2):
                        last = pe.matmul(banks(4 + 2 * which + h, 1), W["w_xdbl"][:, k, which * P:(which + 1) * P],
                                         U[:, k, h * HALF:(h + 1) * HALF], start=(k == 0), stop=(k == 2),
                                         skip_group_check=True)
                    return last

                slot = [0]

                def b_slot():
                    if slot[0]:
                        pe.wait_ge(bslot_free.sem, bslot_free.after(b, slot[0]))
                    slot[0] += 1

                def dt_product(s):
                    b_slot()
                    t = TILE_ORDER[s]
                    product(banks(0), [(W["w_dt"][:, 0, t * P:(t + 1) * P], flat(DTS))]
                            ).then_inc(bslot_full.sem, 1)

                def broadcast(dst, i, c):
                    s, n = divmod(i, NST)
                    t = TILE_ORDER[s]
                    return product(dst, [(SEL[:, (t % 3) * NST + n, :], flat(BCS[0:96, 2 * (t // 3) + c, :]))])

                def c_product(i):
                    if i >= 2:
                        pe.wait_ge(hc_ready.sem, hc_ready.after(b, i - 1))
                    broadcast(banks(2 + 2 * (i % 2)), i, 1).then_inc(cslot_full.sem, 1)

                def accumulate(i):
                    pe.wait_ge(hc_ready.sem, hc_ready.after(b, i + 1))
                    pair, k = divmod(i, 2 * NST)
                    if k == 0 and pair:
                        pe.wait_ge(y_saved.sem, y_saved.after(b, pair))
                    for h in range(2):
                        last = pe.matmul(banks(6)[:, h * HALF:(h + 1) * HALF], W["ident"][:, 0, :],
                                         HC[:, i % R_HC, h * HALF:(h + 1) * HALF],
                                         start=(k == 0), stop=(k == 2 * NST - 1), skip_group_check=True)
                    last.then_inc(acc_done.sem, 1)

                pe.wait_ge(z_read.sem, z_read.after(b, 1))
                pe.wait_ge(u_ready.sem, u_ready.after(b, 1))
                x_proj(0, 0)
                x_proj(1, 0)
                pe.wait_ge(u_ready.sem, u_ready.after(b, 2))
                x_proj(0, 1)
                x_proj(0, 2).then_inc(xdbl_psum.sem, 1)
                x_proj(1, 1)
                x_proj(1, 2).then_inc(xdbl_psum.sem, 1)
                pe.wait_ge(dts_saved.sem, dts_saved.after(b, 1))
                dt_product(0)
                pe.wait_ge(consts.sem, 16 * N_CONST)
                pe.wait_ge(bcs_loaded.sem, bcs_loaded.after(b, 12))
                for i in range(ITEMS):
                    s, n = divmod(i, NST)
                    b_slot()
                    broadcast(banks(0), i, 0).then_inc(bslot_full.sem, 1)
                    if n == DT_AT and s < SEQ - 1:
                        dt_product(s + 1)
                    if i >= C_LAG:
                        c_product(i - C_LAG)
                    if i >= ACC_LAG:
                        accumulate(i - ACC_LAG)
                def bank(k, h):
                    return banks(2 * k + h, 1)

                low, high, idn = W["to_low"][:, 0, :], W["to_high"][:, 0, :], W["ident"][:, 0, :]

                def add_sums(dst, h, lhs, rhs, start=False, stop=False):
                    return pe.matmul(dst, lhs, rhs(h), start=start, stop=stop, skip_group_check=True)

                for i in range(ITEMS, ITEMS + ACC_LAG):
                    if i - C_LAG < ITEMS:
                        c_product(i - C_LAG)
                    accumulate(i - ACC_LAG)
                    if i == ITEMS:
                        pe.wait_ge(bslot_free.sem, bslot_free.after(b, ITEMS + SEQ))
                        for h in range(2):
                            add_sums(bank(0, h), h, idn, flat(YSB[:, 0, :]), start=True)
                    elif i == ITEMS + 1:
                        for h in range(2):
                            add_sums(bank(0, h), h, low, turned(YSB[:, 1, :]))
                    elif i == ITEMS + 2:
                        pe.wait_ge(hc_ready.sem, hc_ready.after(b, ITEMS - 1))
                        for h in range(2):
                            add_sums(bank(1, h)[0:XT, :], h, idn[:, 0:XT], flat(YSB[:, 1, :]), start=True)

                pe.wait_ge(y_saved.sem, y_saved.after(b, 3))
                for h in range(2):
                    add_sums(bank(0, h), h, high, turned(YSB[:, 2, :]), stop=True)
                    add_sums(bank(1, h)[0:XT, :], h, low[:, 0:XT], turned(YSB[:, 2, :]), stop=True
                             ).then_inc(y_psum.sem, 1)
                cm = W["chan_mean"][:, 0, :]
                for h in range(2):
                    pe.wait_ge(yf_ready.sem, yf_ready.after(b, h + 1))
                    half_product(bank(2, h), h, [(cm, flat(YF[:, 0, :])), (cm[0:XT, :], flat(YF[0:XT, 1, :]))]
                                 ).then_inc(mean_psum.sem, 1)
                for h in range(2):
                    pe.wait_ge(sq_ready.sem, sq_ready.after(b, h + 1))
                    half_product(bank(3, h), h, [(cm, flat(SQ[:, 0, :])), (cm[0:XT, :], flat(SQ[0:XT, 1, :]))]
                                 ).then_inc(var_psum.sem, 1)
                for h in range(2):
                    pe.wait_ge(yg_ready.sem, yg_ready.after(b, h + 1))
                    for m in range(CT):
                        last = half_product(bank(m, h), h, [
                            (W["w_out"][:, 0, m * P:(m + 1) * P], flat(YF[:, 0, :])),
                            (W["w_out"][0:XT, 1, m * P:(m + 1) * P], flat(YF[0:XT, 1, :]))])
                        last.then_inc(op_psum.sem, 1)

                group_stats(gn_stats, gn_psum, 1, 6)
                pe.wait_ge(xn_ready.sem, xn_ready.after(b, 1))
                pe.wait_ge(att_loaded.sem, att_loaded.after(b, len(ATT_MATS)))

                def value_product(t, k):
                    if t >= 4 and k == 0:
                        pe.wait_ge(v_saved.sem, v_saved.after(b, t - 3))
                    last = pe.matmul(banks(t % 4, 1)[:, 0:C], XN[:, k, t * P:(t + 1) * P],
                                     W["w_qkv"][:, k, 2 * C:3 * C], start=(k == 0), stop=(k == CT - 1))
                    if k == CT - 1:
                        last.then_inc(v_psum.sem, 1)

                job_saved = {"proj": raw_saved, "turn": sin_done, "rel": rel_saved}

                def job(phase, m, blocks=()):
                    kind, n = JOBS[phase][m]
                    between = [(t, k) for t in blocks for k in range(CT)]
                    if phase or m >= 4:
                        before, k = JOBS[0][m - 4] if phase == 0 else \
                            JOBS[phase][m - 1] if m else JOBS[phase - 1][-1]
                        pe.wait_ge(job_saved[before].sem, job_saved[before].after(b, k + 1))
                    dst = banks(job_bank(phase, m), 1)
                    if kind == "proj":
                        tensor, h = divmod(n, 2)
                        g, side = PREPARED[tensor]
                        c0 = "qk".index(side) * C + g * P
                        if n == 1:
                            pe.wait_ge(xn_ready.sem, xn_ready.after(b, 2))
                        half_product(dst, h, [(W["w_qkv"][:, k, c0:c0 + P], xn[k]) for k in range(CT)]
                                     ).then_inc(proj_psum.sem, 1)
                    elif kind == "turn":
                        pe.wait_ge(raw_saved.sem, raw_saved.after(b, n + 1))
                        pe.matmul(dst, W["turn"][:, 0, :], RAW[n if n < 4 else n % 2], start=True, stop=True
                                  ).then_inc(turn_psum.sem, 1)
                    else:
                        pe.wait_ge(rope_ready.sem, rope_ready.after(b, 2 if n < 4 else 8))
                        axis, part = divmod(n, 2) if n < 4 else divmod(n - 4, 4)
                        groups, lines = (1, IMG // 2) if n < 4 else (2, IMG // 4)
                        grid = QKC[:, 0:2 * groups - 1:2, :].rearrange("p g (h w) -> p g h w", h=IMG)
                        mat = W[("rel_h", "rel_w")[axis]][:, 0, :]
                        for r in range(lines):
                            at = part * lines + r
                            last = pe.matmul(dst[:, r * groups * IMG:(r + 1) * groups * IMG],
                                             mat[:, HG * (IMG - 1 - at):HG * (REL - at)],
                                             grid[:, :, at, :] if axis == 0 else grid[:, :, :, at],
                                             start=True, stop=True, skip_group_check=True)
                            if between and r % (lines // (CT * len(blocks) + 1)) == 1:
                                value_product(*between.pop(0))
                        last.then_inc(rel_psum.sem, 1)
                    for t, k in between:
                        value_product(t, k)

                def scores(s):
                    g, k = divmod(s, STEPS)
                    qb, j = divmod(k, HG)
                    if qb == 0:
                        pe.wait_ge(head_loaded[j].sem, head_loaded[j].after(b, 4 * (g + 1)))
                    if s >= 2:
                        pe.wait_ge(exp_done.sem, exp_done.after(b, s - 1))
                    product(banks(2 * (s % 2)), [(QX[0:3 * HD, j, qb * P:(qb + 1) * P], flat(KX[0:3 * HD, j, :]))]
                            ).then_inc(s_psum.sem, 1)

                def turn_probs(s):
                    pe.wait_ge(exp_done.sem, exp_done.after(b, s + 1))
                    if s:
                        pe.wait_ge(pt_saved.sem, pt_saved.after(b, s))
                    for t in range(QB):
                        last = pe.transpose(banks(4)[:, t * P:(t + 1) * P], PR[:, s % 2, t * P:(t + 1) * P], idn)
                    last.then_inc(pt_psum.sem, 1)

                def weigh(n):
                    g = n // QB
                    pe.wait_ge(pt_saved.sem, pt_saved.after(b, HG * (n + 1)))
                    if n:
                        pe.wait_ge(o_saved.sem, o_saved.after(b, n))
                    for t in range(QB):
                        for j in range(HG):
                            head = HG * g + j
                            last = pe.matmul(banks(6, 1)[HD * j:HD * j + HD, (n % 2) * P:(n % 2 + 1) * P],
                                             V[:, t, head * HD:(head + 1) * HD], PT[:, n % 2, j, t, :],
                                             start=(t == 0), stop=(t == QB - 1), skip_group_check=True)
                    last.then_inc(o_psum.sem, 1)

                def late(job):
                    if job[0] == "sums":
                        k, h = divmod(job[1], 2)
                        heads = slice(0, 2 * HG) if k == 0 else slice(2 * HG, 3 * HG)
                        pe.wait_ge(rs_ready.sem, rs_ready.after(b, 1 if k == 0 else h + 2))
                        if job[1] == 0:
                            pe.wait_ge(sin_done.sem, sin_done.after(b, 4 * GROUPS))
                        elif job[1] == 3:
                            pe.wait_ge(pj_read.sem, pj_read.after(b, CT))
                        else:
                            pe.wait_ge(on_ready.sem, on_ready.after(b, 2 if job[1] == 1 else 4))
                        if job[1] == 2:
                            pe.wait_ge(xn_ready.sem, xn_ready.after(b, 3))
                        for t in range(QB // 2):
                            last = pe.transpose(banks(7, 1)[0:heads.stop - heads.start, t * P:(t + 1) * P],
                                                row_sum[:, h * QB // 2 + t, heads], idn)
                        last.then_inc(rt_psum.sem, 1)
                    elif job[0] == "norm":
                        g, h = job[1:]
                        pe.wait_ge(rt_saved.sem, rt_saved.after(b, h + 1 if g < 2 else h + 3))
                        if g == 1:
                            pe.wait_ge(on_ready.sem, on_ready.after(b, norm_count(g, h) - 1))
                        rows, at = (2 * HG, g * P) if g < 2 else (HG, 0)
                        pe.matmul(banks(7, 1), W["head_rows"][0:rows, 0, at:at + P],
                                  RT[0:rows, h * HALF:(h + 1) * HALF],
                                  start=True, stop=True).then_inc(rb_psum.sem, 1)
                    elif job[0] == "next":
                        pe.wait_ge(on_ready.sem, on_ready.after(b, 4))
                        group_stats(gn_stats, gn_psum, 2, 7)
                    else:
                        m, h = job[1:]
                        pe.wait_ge(on_ready.sem, on_ready.after(b, norm_count(2, h)))
                        if m:
                            pe.wait_ge(pj_read.sem, pj_read.after(b, m))
                        half_product(banks(7, 1), h, [(W["w_proj"][:, k, m * P:(m + 1) * P], flat(OT[:, k, :]))
                                                      for k in range(CT)]).then_inc(pj_psum.sem, 1)

                def project(m, ks):
                    for k in ks:
                        last = pe.matmul(banks(m, 1), W["w_proj"][:, k, m * P:(m + 1) * P], OT[:, k, HALF:L],
                                         start=(k == 0), stop=(k == CT - 1), skip_group_check=True)
                    return last

                for m, blocks in START:
                    if m is None:
                        for t in blocks:
                            for k in range(CT):
                                value_product(t, k)
                    else:
                        job(0, m, blocks)
                pe.wait_ge(v_saved.sem, v_saved.after(b, QB))
                pe.wait_ge(onehot_loaded.sem, onehot_loaded.after(b, HG))
                scores(0)
                for s in range(STEPS * GROUPS):
                    g, k = divmod(s, STEPS)
                    if s + 1 < STEPS * GROUPS:
                        scores(s + 1)
                    if k in JOB_AT[g]:
                        job(g + 1, JOB_AT[g][k])
                    if g + 1 == GROUPS and k in LATE_AT:
                        late(LATE_AT[k])
                    if s % HG == 1 and s > HG:
                        weigh(s // HG - 1)
                    if s + 1 == STEPS * GROUPS:
                        pe.wait_ge(exp_done.sem, exp_done.after(b, s))
                        project(0, (0, 1))
                        project(1, (0, 1))
                    turn_probs(s)

                late(("sums", 3))
                project(2, (0, 1))
                late(("norm", 2, 1))
                weigh(QB * GROUPS - 1)
                pe.wait_ge(on_ready.sem, on_ready.after(b, 2 * GROUPS))
                for m in range(CT):
                    project(m, (2,)).then_inc(pj_psum.sem, 1)
                conv_input()
                leave_image(pe, b)

        @block.vector
        def _(dve):
            dve.memset(one[:, :], 1.0)
            dve.memset(eps[:, :], LN_EPS)
            dve.wait_ge(columns.sem, 16 * N_COLUMNS)
            dve.tensor_scalar(a_inf[:, :], COL["a_log"][:, :], A_LOG_MAX, -200.0, ALU.is_gt, ALU.mult)
            dve.tensor_scalar(a_low[:, :], COL["a_log"][:, :], A_LOG_MAX, None, ALU.min).then_inc(prep.sem, 1)
            sk = COL["skip"][:, :].rearrange("p (m k) -> p m k", m=2)
            dve.tensor_reduce(skip_sum[:, :], sk, AX_X, ALU.add).then_inc(prep.sem, 1)
            dve.tensor_scalar(bk_scaled[:, :], COL["b_qkv"][:, 3:6], ATT_SCALE, None, ALU.mult).then_inc(prep.sem, 1)
            dve.wait_ge(prep.sem, 4)
            dve.wait_ge(first_x.sem, first_x.after(0, 1))

            def half_stats(src, h):
                for k in range(CT):
                    last = dve.bn_stats(bn[:, k, h, :], src[:, k, h * HALF:(h + 1) * HALF])
                return last

            def group_moments(link, stats):
                for k in range(CT):
                    last = dve.bn_aggr(mv[:, k, :], bn[:, k, :, :])
                link(last)
                link(dve.tensor_tensor(g_tmp[:, :], mv[:, :, 0], mv[:, :, 0], ALU.mult))
                dve.tensor_tensor(mv[:, :, 1], mv[:, :, 1], g_tmp[:, :], ALU.add).then_inc(stats.sem, 1)

            def group_variance(link, psum, var, n, bank):
                dve.wait_ge(psum.sem, n)
                link(dve.tensor_copy(gs[:, :, :], PS[:, bank * HALF:bank * HALF + 2 * CT].rearrange(
                    "p (m t) -> p m t", t=2)))
                link(dve.tensor_tensor(g_tmp[:, :], gs[:, :, 0], gs[:, :, 0], ALU.mult))
                link(dve.tensor_tensor(g_tmp[:, :], gs[:, :, 1], g_tmp[:, :], ALU.subtract))
                dve.tensor_scalar(g_tmp[:, :], g_tmp[:, :], GN_EPS, None, ALU.add).then_inc(var.sem, 1)

            def normalise(rstd, n, src, at=slice(0, L)):
                dve.wait_ge(rstd.sem, n)
                for k in range(CT):
                    last = dve.tensor_scalar(XN[:, k, at], src[:, k, at], gs[:, k, 0:1], g_rstd[:, k:k + 1],
                                             ALU.subtract, ALU.mult)
                return last

            first_link = steps(dve, first_step, 0)
            half_stats(XN, 0)
            first_link(half_stats(XN, 1))
            group_moments(first_link, first_gn[0])
            group_variance(first_link, first_gn[1], first_gn[2], 1, 7)
            normalise(first_gn[3], 1, XN).then_inc(xn_first.sem, 1)

            with dve.Fori(0, B) as b:
                link = steps(dve, dve_step, b)

                dve.memset(PADDED[0:XT, 0:IMG], 0.0)
                dve.memset(PADDED[XT:P, (IMG // 2 + 1) * IMG:(IMG // 2 + 2) * IMG], 0.0).then_inc(pads_zero.sem, 1)

                grid = banks(4).rearrange("p (h w) -> p h w", h=IMG)
                padded = PADDED.rearrange("p (h w) -> p h w", w=IMG)
                wc = COL["conv_w"]
                for m, src, rows in ((0, grid, IMG), (1, padded, IMG // 2)):
                    dve.wait_ge(centre_done.sem, centre_done.after(b, m + 1))
                    if m:
                        dve.wait_ge(pads_zero.sem, pads_zero.after(b, 1))
                    acc = CONV[:, m, 0:rows * IMG].rearrange("p (h w) -> p h w", w=IMG)
                    last = None
                    for tap in [0, 1, 2, 3, 5, 6, 7, 8]:
                        if last is not None:
                            link(last)
                        dy, dx = tap // 3 - 1, tap % 3 - 1
                        y0, y1 = (0, rows) if m else (max(0, -dy), rows - max(0, dy))
                        x0, x1 = max(0, -dx), IMG - max(0, dx)
                        dst = acc[:, y0:y1, x0:x1]
                        last = dve.scalar_tensor_tensor(
                            out=dst, in0=src[:, y0 + dy + m:y1 + dy + m, x0 + dx:x1 + dx],
                            scalar=wc[:, 9 * m + tap:9 * m + tap + 1], in1=dst, op0=ALU.mult, op1=ALU.add)
                    last.then_inc(conv_done.sem, 1)

                dve.wait_ge(bc_hi.sem, bc_hi.after(b, 1))
                link(dve.tensor_tensor(REST[:, 0, :], banks(6), BCP[:, 0, :], ALU.subtract))
                dve.tensor_copy(BCP[:, 1, :], REST[:, 0, :]).then_inc(bc_mid.sem, 1)
                dve.wait_ge(bc_mid.sem, bc_mid.after(b, 1))
                link(dve.tensor_tensor(REST[:, 1, :], REST[:, 0, :], BCP[:, 1, :], ALU.subtract))
                dve.tensor_copy(BCP[:, 2, :], REST[:, 1, :]).then_inc(bc_split.sem, 1)

                def soft_series(s):
                    dve.wait_ge(soft_e.sem, soft_e.after(b, s + 1))
                    dve.tensor_scalar(MASK, SE, SMALL, None, ALU.is_lt)
                    dve.scalar_tensor_tensor(out=SQ3, in0=SE, scalar=-1.5, in1=SE, op0=ALU.add,
                                             op1=ALU.mult).then_inc(soft_q2.sem, 1)

                def soft_series_end(s):
                    dve.wait_ge(soft_q2.sem, soft_q2.after(b, s + 1))
                    dve.scalar_tensor_tensor(out=SQ3, in0=SQ3, scalar=3.0, in1=SE, op0=ALU.add,
                                             op1=ALU.mult).then_inc(soft_q.sem, 1)

                def soft_pick(s):
                    dve.wait_ge(soft_ln.sem, soft_ln.after(b, s + 1))
                    dve.wait_ge(soft_q3.sem, soft_q3.after(b, s + 1))
                    dve.copy_predicated(DELTA[:, s % 2, :], MASK, SQ3).then_inc(soft_log.sem, 1)

                def scan(i):
                    s = i // NST
                    dve.wait_ge(da_ready.sem, da_ready.after(b, i + 1))
                    dve.wait_ge(dbu_ready.sem, dbu_ready.after(b, i + 1))
                    if i >= 2:
                        dve.wait_ge(hc_ready.sem, hc_ready.after(b, i - 1))
                    step = 1 if TILE_ORDER[s] < 3 else -1
                    dve.tensor_tensor_scan(HS[:, i % 2, ::step], DA[:, i % 3, ::step], DBU[:, i % R3, ::step],
                                           0.0, ALU.mult, ALU.add).then_inc(scan_done.sem, 1)

                def times_c(i):
                    dve.wait_ge(scan_done.sem, scan_done.after(b, i + 1))
                    dve.wait_ge(cslot_full.sem, cslot_full.after(b, i + 1))
                    if i >= R_HC:
                        dve.wait_ge(acc_done.sem, acc_done.after(b, i - R_HC + 1))
                    dve.tensor_tensor(HC[:, i % R_HC, :], HS[:, i % 2, :], banks(2 + 2 * (i % 2)), ALU.mult
                                      ).then_inc(hc_ready.sem, 1)

                soft_series(0)
                soft_series_end(0)
                dve.wait_ge(soft_q.sem, soft_q.after(b, 1))
                dve.tensor_scalar(SQ3, SQ3, 1.0 / 3.0, None, ALU.mult).then_inc(soft_q3.sem, 1)
                soft_pick(0)
                dve.wait_ge(soft_log.sem, soft_log.after(b, 1))
                dve.tensor_tensor(DELTA[:, 0, :], DELTA[:, 0, :], SR, ALU.add).then_inc(delta_ready.sem, 1)
                dve.wait_ge(delta_ready.sem, delta_ready.after(b, 1))
                dve.tensor_tensor(DU[:, 0, :], DELTA[:, 0, :], U[:, TILE_ORDER[0] % 3, :], ALU.mult
                                  ).then_inc(du_ready.sem, 1)
                dve.wait_ge(du_ready.sem, du_ready.after(b, 1))
                dve.wait_ge(bslot_free.sem, bslot_free.after(b, 1 + dt_before(0)))
                dve.tensor_tensor(DBU[:, 0, :], DU[:, 0, :], BSB[:, 0, :], ALU.mult).then_inc(dbu_ready.sem, 1)
                for i in range(ITEMS):
                    s, n = divmod(i, NST)
                    scan(i)
                    if i:
                        times_c(i - 1)
                    if s < SEQ - 1 and n == SERIES_AT:
                        soft_series(s + 1)
                    if s < SEQ - 1 and n == SERIES_END_AT:
                        soft_series_end(s + 1)
                    if s < SEQ - 1 and n == PICK_AT:
                        soft_pick(s + 1)
                times_c(ITEMS - 1)

                def half(h):
                    return slice(h * HALF, (h + 1) * HALF)

                def bank(k, h):
                    return banks(2 * k + h, 1)

                for h in range(2):
                    dve.wait_ge(y_psum.sem, y_psum.after(b, h + 1))
                    for m, rows in ((0, P), (1, XT)):
                        last = dve.scalar_tensor_tensor(out=YF[0:rows, m, half(h)], in0=U[0:rows, m, half(h)],
                                                        scalar=skip_sum[0:rows, m:m + 1], in1=bank(m, h)[0:rows, :],
                                                        op0=ALU.mult, op1=ALU.add)
                    last.then_inc(yf_ready.sem, 1)
                for h in range(2):
                    dve.wait_ge(yf_ready.sem, yf_ready.after(b, h + 1))
                    dve.wait_ge(mean_psum.sem, mean_psum.after(b, h + 1))
                    for m, rows in ((0, P), (1, XT)):
                        last = dve.tensor_tensor(YF[0:rows, m, half(h)], YF[0:rows, m, half(h)], bank(2, h)[0:rows, :],
                                                 ALU.subtract)
                    last.then_inc(yc_ready.sem, 1)
                for h in range(2):
                    dve.wait_ge(rstd_ready.sem, rstd_ready.after(b, h + 1))
                    for m, rows in ((0, P), (1, XT)):
                        last = dve.scalar_tensor_tensor(
                            out=YF[0:rows, m, half(h)], in0=YF[0:rows, m, half(h)],
                            scalar=COL["norm_g"][0:rows, m:m + 1],
                            in1=RSTD[0:rows, half(h)], op0=ALU.mult, op1=ALU.mult)
                    link(last)
                    for m, rows in ((0, P), (1, XT)):
                        last = dve.scalar_tensor_tensor(
                            out=YF[0:rows, m, half(h)], in0=YF[0:rows, m, half(h)],
                            scalar=COL["norm_b"][0:rows, m:m + 1],
                            in1=ZS[0:rows, m, half(h)], op0=ALU.add, op1=ALU.mult)
                    last.then_inc(yg_ready.sem, 1)
                dve.wait_ge(x_loaded.sem, x_loaded.after(b, 1))
                for k in range(2 * CT + 1):
                    if k < 2 * CT:
                        h, m = divmod(k, CT)
                        dve.wait_ge(op_psum.sem, op_psum.after(b, k + 1))
                        dve.tensor_tensor(X[:, m, half(h)], X[:, m, half(h)], bank(m, h), ALU.add
                                          ).then_inc(x_added.sem, 1)
                    if k:
                        h, m = divmod(k - 1, CT)
                        dve.wait_ge(x_added.sem, x_added.after(b, k))
                        last = dve.bn_stats(bn[:, m, h, :], X[:, m, half(h)])
                link(last)

                group_moments(link, gn_stats)
                group_variance(link, gn_psum, gn_var, 1, 6)
                for h in range(2):
                    normalise(gn_rstd, 1, X, half(h)).then_inc(xn_ready.sem, 1)

                def job(phase, m):
                    kind, n = JOBS[phase][m]
                    src = banks(job_bank(phase, m), 1)
                    if kind == "turn":
                        h = n % 2
                        dve.wait_ge(turn_psum.sem, turn_psum.after(b, n + 1))
                        if n >= 2:
                            dve.wait_ge(rope_ready.sem, rope_ready.after(b, n - 1))
                        dve.tensor_tensor(RT2[:, h, :], src, W["sin"][:, 0, half(h)], ALU.mult
                                          ).then_inc(sin_done.sem, 1)
                    elif kind == "rel":
                        dve.wait_ge(rel_psum.sem, rel_psum.after(b, n + 1))
                        if n == 4:
                            for loaded in head_loaded:
                                dve.wait_ge(loaded.sem, loaded.after(b, 4))
                        axis, part = divmod(n, 2) if n < 4 else divmod(n - 4, 4)
                        groups, lines = (1, IMG // 2) if n < 4 else (2, IMG // 4)
                        at = slice(part * lines, (part + 1) * lines)
                        dst = RELC[:, 0:groups, axis, :].rearrange("p g (h w) -> p g h w", h=IMG)
                        if axis == 0:
                            dst, order = dst[:, :, at, :], "p (h g w) -> p g h w"
                            sizes = {"g": groups, "w": IMG}
                        else:
                            dst, order = dst[:, :, :, at], "p (w g h) -> p g h w"
                            sizes = {"g": groups, "h": IMG}
                        src = src.rearrange(order, **sizes)
                        for g in range(groups):
                            last = dve.tensor_copy(dst[:, g], src[:, g])
                        last.then_inc(rel_saved.sem, 1)

                def save_turned(s):
                    n = s // HG
                    dve.wait_ge(pt_psum.sem, pt_psum.after(b, s + 1))
                    if n >= 2:
                        dve.wait_ge(o_psum.sem, o_psum.after(b, n - 1))
                    dve.tensor_copy(PT[:, n % 2, s % HG, :, :], banks(4).rearrange("p (t q) -> p t q", t=QB)
                                    ).then_inc(pt_saved.sem, 1)

                def late(job):
                    if job[0] == "sums":
                        k, h = divmod(job[1], 2)
                        rows = (2 * HG, HG)[k]
                        dve.wait_ge(rt_psum.sem, rt_psum.after(b, job[1] + 1))
                        if job[1] == 0:
                            for loaded in head_loaded:
                                dve.wait_ge(loaded.sem, loaded.after(b, 4 * GROUPS))
                        dve.tensor_copy(RT[0:rows, half(h)], banks(7, 1)[0:rows, :]).then_inc(rt_saved.sem, 1)
                    elif job[0] == "norm":
                        g, h = job[1:]
                        dve.wait_ge(rb_psum.sem, rb_psum.after(b, norm_count(g, h)))
                        dve.wait_ge(o_saved.sem, o_saved.after(b, QB * g + QB // 2 * (h + 1)))
                        link(dve.tensor_tensor(OT[:, g, half(h)], OT[:, g, half(h)], banks(7, 1), ALU.mult))
                        dve.tensor_scalar(OT[:, g, half(h)], OT[:, g, half(h)], COL["b_qkv"][:, 6 + g:7 + g], None,
                                          ALU.add).then_inc(on_ready.sem, 1)
                    elif job[0] == "next":
                        group_variance(link, gn_psum, gn_var, 2, 7)
                    else:
                        m, h = job[1:]
                        dve.wait_ge(pj_psum.sem, pj_psum.after(b, CT * h + m + 1))
                        dve.scalar_tensor_tensor(out=OUT[:, m, half(h)], in0=banks(7 if h == 0 else m, 1),
                                                 scalar=COL["b_proj"][:, m:m + 1], in1=X[:, m, half(h)],
                                                 op0=ALU.add, op1=ALU.add).then_inc(pj_read.sem, 1)

                def invert_sums(which):
                    last_step = (2 * STEPS, 2 * STEPS + STEPS // 2, 3 * STEPS)[which]
                    rows = row_sum[:, :, 0:2 * HG] if which == 0 else \
                        row_sum[:, (which - 1) * QB // 2:which * QB // 2, 2 * HG:3 * HG]
                    dve.wait_ge(exp_done.sem, exp_done.after(b, last_step))
                    dve.reciprocal(rows, rows).then_inc(rs_ready.sem, 1)

                for m in range(len(JOBS[0])):
                    job(0, m)
                for s in range(STEPS * GROUPS):
                    g, k = divmod(s, STEPS)
                    dve.wait_ge(s_psum.sem, s_psum.after(b, s + 1))
                    if s >= 4:
                        dve.wait_ge(exp_done.sem, exp_done.after(b, s - 3))
                    dve.tensor_reduce(neg_max[:, s % 4:s % 4 + 1], banks(2 * (s % 2)), AX_X, ALU.max,
                                      negate=True).then_inc(max_done.sem, 1)
                    if k - 1 in JOB_AT[g]:
                        job(g + 1, JOB_AT[g][k - 1])
                    if g + 1 == GROUPS and k - 1 in LATE_AT:
                        late(LATE_AT[k - 1])
                    if g + 1 == GROUPS:
                        if k == 1:
                            invert_sums(0)
                        elif k in (8, 10):
                            if k == 8:
                                dve.wait_ge(next_loaded.sem, next_loaded.after(b, 5))
                            link(half_stats(XN, (k - 8) // 2))
                        elif k == 12:
                            group_moments(link, gn_stats)
                        elif k == 17:
                            normalise(gn_rstd, 2, XN).then_inc(xn_ready.sem, 1)
                        elif k == STEPS // 2 + 2:
                            invert_sums(1)
                    if s % 2 == 1:
                        save_turned(s - 1)

                invert_sums(2)
                for job_ in (("sums", 3), ("norm", 2, 1), ("proj", 0, 1), ("proj", 1, 1), ("proj", 2, 1)):
                    late(job_)
                leave_image(dve, b)

        @block.scalar
        def _(act):
            act.wait_ge(columns.sem, 16 * N_COLUMNS)
            act.wait_ge(prep.sem, 1)
            act.activation(a_neg[:, :], a_low[:, :], ACT.Exp).then_inc(a_exp, 1)
            act.wait_ge(a_exp, 1)
            act.mul(a_neg[:, :], a_neg[:, :], -1.0).then_inc(prep.sem, 1)
            act.wait_ge(prep.sem, 4)

            act.preload_act_table_set("natural_log_exp_and_others")
            act.wait_ge(first_gn[2].sem, 1)
            act.activation(g_rstd[:, :], g_tmp[:, :], ACT.Ln).then_inc(a_exp, 1)
            act.wait_ge(a_exp, 2)
            act.activation(g_rstd[:, :], g_rstd[:, :], ACT.Exp, scale=-0.5).then_inc(first_gn[3].sem, 1)

            with act.Fori(0, B) as b:
                link = steps(act, act_step, b)
                def by_column(ap):
                    return ap.rearrange("p (h w) -> p w h", h=IMG)

                def grid(ap):
                    return ap.rearrange("p (w h) -> p w h", h=IMG)

                for m, src in ((0, banks(4)), (1, PADDED[:, IMG:(IMG // 2 + 1) * IMG])):
                    if m == 0:
                        act.wait_ge(conv_input_done, b + 1)
                    else:
                        act.wait_ge(xh_psum.sem, xh_psum.after(b, 1))
                    act.activation(CONV[:, m, 0:src.shape[1]], src, ACT.Identity, bias=COL["conv_b"][:, m:m + 1],
                                   scale=COL["conv_w"][:, 9 * m + 4:9 * m + 5]).then_inc(centre_done.sem, 1)
                act.wait_ge(conv_done.sem, conv_done.after(b, 1))
                act.activation(U[:, 0, :], CONV[:, 0, :], ACT.Silu).then_inc(u_ready.sem, 1)
                act.wait_ge(z_psum.sem, z_psum.after(b, 1))
                act.activation(ZS[:, 0, :], banks(0), ACT.Silu)
                act.activation(ZS[0:XT, 1, :], banks(6)[0:XT, :], ACT.Silu).then_inc(z_read.sem, 1)
                act.activation(grid(U[XT:P, 1, :]), by_column(CONV[0:XT, 0, :]), ACT.Silu)
                act.activation(grid(U[0:XT, 2, :]), by_column(CONV[XT:P, 0, :]), ACT.Silu)
                act.wait_ge(conv_done.sem, conv_done.after(b, 2))
                for h in range(2):
                    src = CONV[XT * h:XT * h + XT, 1, 0:HALF]
                    act.activation(U[0:XT, 1, h * HALF:(h + 1) * HALF], src, ACT.Silu)
                    last = act.activation(grid(U[XT:P, 2, :])[:, :, h * (IMG // 2):(h + 1) * (IMG // 2)],
                                          src.rearrange("p (h w) -> p w h", w=IMG), ACT.Silu)
                last.then_inc(u_ready.sem, 1)
                act.preload_act_table_set("natural_log_exp_and_others")
                act.wait_ge(xdbl_psum.sem, xdbl_psum.after(b, 1))
                act.activation(DTS, banks(4), ACT.Copy).then_inc(dts_saved.sem, 1)
                slot = [0]

                def soft(s):
                    t = TILE_ORDER[s]
                    slot[0] += 1
                    act.wait_ge(bslot_full.sem, bslot_full.after(b, slot[0]))
                    bias = COL["dt_b"][:, t:t + 1]
                    if s:
                        act.wait_ge(delta_ready.sem, delta_ready.after(b, s))
                    link(act.activation(SE, banks(0), ACT.Abs, bias=bias))
                    act.activation(SR, banks(0), ACT.Relu, bias=bias).then_inc(bslot_free.sem, 1)

                def soft_exp(s):
                    act.activation(SE, SE, ACT.Exp, scale=-1.0).then_inc(soft_e.sem, 1)

                def soft_log1p(s):
                    act.wait_ge(soft_e.sem, soft_e.after(b, s + 1))
                    act.activation(DELTA[:, s % 2, :], SE, ACT.Ln, bias=one[:, 0:1]).then_inc(soft_ln.sem, 1)

                def soft_third(s):
                    act.wait_ge(soft_q.sem, soft_q.after(b, s + 1))
                    act.activation(SQ3, SQ3, ACT.Copy, scale=1.0 / 3.0).then_inc(soft_q3.sem, 1)

                def decay(i):
                    s, n = divmod(i, NST)
                    if n == 0:
                        act.wait_ge(delta_ready.sem, delta_ready.after(b, s + 1))
                    if i >= 3:
                        act.wait_ge(scan_done.sem, scan_done.after(b, i - 2))
                    at = TILE_ORDER[s] * NST + n
                    act.activation(DA[:, i % 3, :], DELTA[:, s % 2, :], ACT.Exp, bias=a_inf[:, at:at + 1],
                                   scale=a_neg[:, at:at + 1]).then_inc(da_ready.sem, 1)

                act.wait_ge(xdbl_psum.sem, xdbl_psum.after(b, 2))
                act.activation(BCP[:, 0, :], banks(6), ACT.Copy).then_inc(bc_hi.sem, 1)
                soft(0)
                soft_exp(0)
                soft_log1p(0)
                for i in range(ITEMS):
                    s, n = divmod(i, NST)
                    slot[0] += 1
                    act.wait_ge(bslot_full.sem, bslot_full.after(b, slot[0]))
                    if i >= R3:
                        act.wait_ge(dbu_ready.sem, dbu_ready.after(b, i - R3 + 1))
                    act.activation(BSB[:, i % R3, :], banks(0), ACT.Copy).then_inc(bslot_free.sem, 1)
                    decay(i)
                    if n == DT_AT and s < SEQ - 1:
                        soft(s + 1)
                    if n == EXP_AT and s < SEQ - 1:
                        soft_exp(s + 1)
                    if n == LN_AT and s < SEQ - 1:
                        soft_log1p(s + 1)
                    if n == THIRD_AT and s < SEQ - 1:
                        soft_third(s + 1)
                    pair, k = divmod(i, 2 * NST)
                    if (k == ACC_LAG - 1 and pair) or i == ITEMS - 1:
                        done = pair if i != ITEMS - 1 else pair + 1
                        act.wait_ge(acc_done.sem, acc_done.after(b, 2 * NST * done))
                        act.activation(YSB[:, done - 1, :], banks(6), ACT.Copy).then_inc(y_saved.sem, 1)

                def half(h):
                    return slice(h * HALF, (h + 1) * HALF)

                for h in range(2):
                    act.wait_ge(yc_ready.sem, yc_ready.after(b, h + 1))
                    act.activation(SQ[:, 0, half(h)], YF[:, 0, half(h)], ACT.Square)
                    act.activation(SQ[0:XT, 1, half(h)], YF[0:XT, 1, half(h)], ACT.Square).then_inc(sq_ready.sem, 1)
                for h in range(2):
                    act.wait_ge(var_psum.sem, var_psum.after(b, h + 1))
                    link(act.activation(RSTD[:, half(h)], banks(6 + h, 1), ACT.Ln, bias=eps[:, 0:1]))
                    act.activation(RSTD[:, half(h)], RSTD[:, half(h)], ACT.Exp, scale=-0.5).then_inc(rstd_ready.sem, 1)

                def group_rstd(n):
                    act.wait_ge(gn_var.sem, gn_var.after(b, n))
                    link(act.activation(g_rstd[:, :], g_tmp[:, :], ACT.Ln))
                    act.activation(g_rstd[:, :], g_rstd[:, :], ACT.Exp, scale=-0.5).then_inc(gn_rstd.sem, 1)

                group_rstd(1)

                def save_v(t):
                    act.wait_ge(v_psum.sem, v_psum.after(b, t + 1))
                    act.activation(V[:, t, :], banks(t % 4, 1)[:, 0:C], ACT.Copy).then_inc(v_saved.sem, 1)

                def job(phase, m):
                    kind, n = JOBS[phase][m]
                    if kind != "proj":
                        return
                    act.wait_ge(proj_psum.sem, proj_psum.after(b, n + 1))
                    if n >= 4:
                        act.wait_ge(turn_psum.sem, turn_psum.after(b, last_use(n) + 1))
                        act.wait_ge(cos_done.sem, cos_done.after(b, last_use(n) + 1))
                    g, side = PREPARED[n // 2]
                    bias = COL["b_qkv"][:, g:g + 1] if side == "q" else bk_scaled[:, g:g + 1]
                    act.activation(RAW[n if n < 4 else n % 2], banks(job_bank(phase, m), 1), ACT.Identity, bias=bias,
                                   scale=1.0 if side == "q" else ATT_SCALE).then_inc(raw_saved.sem, 1)

                def save_turned(s):
                    n = s // HG
                    act.wait_ge(pt_psum.sem, pt_psum.after(b, s + 1))
                    if n >= 2:
                        act.wait_ge(o_psum.sem, o_psum.after(b, n - 1))
                    act.activation(PT[:, n % 2, s % HG, :, :], banks(4).rearrange("p (t q) -> p t q", t=QB),
                                   ACT.Copy).then_inc(pt_saved.sem, 1)

                def save_sums(n):
                    g, qb = divmod(n, QB)
                    act.wait_ge(o_psum.sem, o_psum.after(b, n + 1))
                    act.activation(OT[:, g, qb * P:(qb + 1) * P], banks(6, 1)[:, (n % 2) * P:(n % 2 + 1) * P],
                                   ACT.Copy).then_inc(o_saved.sem, 1)

                for m, blocks in START:
                    if m is not None:
                        job(0, m)
                    for t in blocks:
                        save_v(t)
                for s in range(STEPS * GROUPS):
                    g, k = divmod(s, STEPS)
                    qb, j = divmod(k, HG)
                    act.wait_ge(max_done.sem, max_done.after(b, s + 1))
                    if s >= 2:
                        act.wait_ge(pt_psum.sem, pt_psum.after(b, s - 1))
                    at = HG * g + j
                    act.activation(PR[:, s % 2, :], banks(2 * (s % 2)), ACT.Exp, bias=neg_max[:, s % 4:s % 4 + 1],
                                   accum_out=row_sum[:, qb, at:at + 1]).then_inc(exp_done.sem, 1)
                    if k - 1 in JOB_AT[g]:
                        job(g + 1, JOB_AT[g][k - 1])
                    if s and s % 2 == 0:
                        save_turned(s - 1)
                    if g + 1 == GROUPS and k == 15:
                        group_rstd(2)
                    if s % HG == 3 and s > HG:
                        save_sums(s // HG - 1)
                save_turned(STEPS * GROUPS - 1)
                save_sums(QB * GROUPS - 1)
                leave_image(act, b)

        @block.gpsimd
        def _(pool):
            with pool.Fori(0, B) as b:
                def delta(s):
                    pool.wait_ge(soft_log.sem, soft_log.after(b, s + 1))
                    pool.tensor_tensor(DELTA[:, s % 2, :], DELTA[:, s % 2, :], SR, ALU.add
                                       ).then_inc(delta_ready.sem, 1)

                def times_u(s):
                    pool.wait_ge(delta_ready.sem, delta_ready.after(b, s + 1))
                    pool.tensor_tensor(DU[:, s % 2, :], DELTA[:, s % 2, :], U[:, TILE_ORDER[s] % 3, :], ALU.mult
                                       ).then_inc(du_ready.sem, 1)

                pool.wait_ge(dbu_ready.sem, dbu_ready.after(b, 1))
                for i in range(1, ITEMS):
                    s, n = divmod(i, NST)
                    if n == 0:
                        pool.wait_ge(du_ready.sem, du_ready.after(b, s + 1))
                    pool.wait_ge(bslot_free.sem, bslot_free.after(b, i + 1 + dt_before(i)))
                    if i >= R3:
                        pool.wait_ge(scan_done.sem, scan_done.after(b, i - R3 + 1))
                    pool.tensor_tensor(DBU[:, i % R3, :], DU[:, s % 2, :], BSB[:, i % R3, :], ALU.mult
                                       ).then_inc(dbu_ready.sem, 1)
                    if s < SEQ - 1 and n == DELTA_AT:
                        delta(s + 1)
                    if s < SEQ - 1 and n == DU_AT:
                        times_u(s + 1)
                pool.wait_ge(att_loaded.sem, att_loaded.after(b, len(ATT_MATS)))
                for n in range(2 * len(PREPARED)):
                    tensor, h = divmod(n, 2)
                    at = slice(h * HALF, (h + 1) * HALF)
                    pool.wait_ge(raw_saved.sem, raw_saved.after(b, n + 1))
                    pool.tensor_tensor(RT1[:, h, :], RAW[n if n < 4 else n % 2], W["cos"][:, 0, at], ALU.mult
                                       ).then_inc(cos_done.sem, 1)
                    pool.wait_ge(cos_done.sem, cos_done.after(b, n + 1))
                    pool.wait_ge(sin_done.sem, sin_done.after(b, n + 1))
                    if n in (4, 10):
                        for loaded in head_loaded:
                            pool.wait_ge(loaded.sem, loaded.after(b, 4 if n == 4 else 8))
                    pool.tensor_tensor(QKC[:, PLACE[PREPARED[tensor]], at], RT1[:, h, :], RT2[:, h, :], ALU.add
                                       ).then_inc(rope_ready.sem, 1)
                leave_image(pool, b)


def dt_before(i):
    s, n = divmod(i, NST)
    return 1 + s + (1 if n > DT_AT and s < SEQ - 1 else 0)


def kernel(x, L0_conv_in_proj_w, L0_conv_conv_w, L0_conv_conv_b, L0_conv_x_proj_w, L0_conv_dt_projs_w,
           L0_conv_dt_projs_b, L0_conv_A_logs, L0_conv_Ds, L0_conv_out_norm_g, L0_conv_out_norm_b,
           L0_conv_out_proj_w, L1_conv_w_qkv, L1_conv_b_qkv, L1_conv_w_proj, L1_conv_b_proj,
           L1_conv_rel_pos_h, L1_conv_rel_pos_w):
    import ml_dtypes
    import numpy as np
    import concourse.bacc as bacc
    from concourse.bass_utils import run_bass_kernel_spmd

    f = np.float32

    def halves(v, twice=False):
        v = np.asarray(v)
        o = np.zeros((P, 2) + v.shape[1:], f)
        o[:, 0] = v[:P]
        o[:XT, 1] = v[P:]
        if twice:
            o[XT:, 1] = v[P:]
        return o

    def tiles(v):
        return np.ascontiguousarray(np.asarray(v).reshape(-1, P).T)

    mats, cols = {}, {}
    mats["w_in"] = np.asarray(L0_conv_in_proj_w).T
    xp = np.asarray(L0_conv_x_proj_w)
    w = np.zeros((2, DI, 2 * P), f)
    for k in range(DIRS):
        order = k % 2
        w[order, :, 32 * k:32 * k + RANK] = xp[k, :RANK].T
        for c in range(2):
            at = P + 64 * (k // 2) + 32 * c + NST * (k % 2)
            w[order, :, at:at + NST] = xp[k, RANK + NST * c:RANK + NST * (c + 1)].T
    mats["w_xdbl"] = np.concatenate([w[0], w[1]])
    wd = np.zeros((P, DIRS * DI), f)
    for k in range(DIRS):
        wd[32 * k:32 * k + RANK, DI * k:DI * (k + 1)] = np.asarray(L0_conv_dt_projs_w)[k].T
    mats["w_dt"] = wd
    wo = np.zeros((2 * P, C), f)
    wo[:DI] = np.asarray(L0_conv_out_proj_w).T
    mats["w_out"] = wo
    mats["w_qkv"] = np.asarray(L1_conv_w_qkv)
    mats["w_proj"] = np.asarray(L1_conv_w_proj)
    ch = np.arange(C)
    mats["group_mean"] = (ch[:, None] // 12 == ch[None, :] // 12) / f(12)
    freqs = (1.0 / np.power(f(10000.0), np.arange(0, HD, 4, dtype=f) / f(HD))).astype(f)
    tok = np.arange(L)
    ang = np.concatenate([(tok % IMG).astype(f)[:, None] * freqs, (tok // IMG).astype(f)[:, None] * freqs], 1)
    rows = (np.arange(P) % HD) // 2
    mats["cos"] = np.cos(ang).T[rows]
    mats["sin"] = np.sin(ang).T[rows]
    mats["ident"] = np.eye(P)
    mats["to_low"] = np.eye(P, k=-XT)
    mats["to_high"] = np.eye(P, k=XT)
    turn = np.zeros((P, P), f)
    for i in range(0, P, 2):
        turn[i + 1, i] = -1.0
        turn[i, i + 1] = 1.0
    mats["turn"] = turn
    mats["chan_mean"] = np.full((P, P), 1.0 / DI)
    hr = np.zeros((NH, C), f)
    hr[ch // HD, ch] = 1.0
    mats["head_rows"] = hr
    for name, table in (("rel_h", L1_conv_rel_pos_h), ("rel_w", L1_conv_rel_pos_w)):
        rel = np.zeros((HG, HD, REL, HG), f)
        for j in range(HG):
            rel[j, :, :, j] = np.asarray(table)[:REL][::-1].T
        mats[name] = rel.reshape(P, HG * REL)

    cols["conv_w"] = halves(np.asarray(L0_conv_conv_w).reshape(DI, 9), twice=True).reshape(P, 18)
    cols["conv_b"] = halves(L0_conv_conv_b, twice=True)
    cols["dt_b"] = tiles(np.asarray(L0_conv_dt_projs_b).reshape(-1))
    cols["a_log"] = np.asarray(L0_conv_A_logs).reshape(SEQ, P, NST).transpose(1, 0, 2).reshape(P, SEQ * NST)
    cols["skip"] = halves(np.asarray(L0_conv_Ds).reshape(DIRS, DI).T).reshape(P, 2 * DIRS)
    cols["norm_g"] = halves(L0_conv_out_norm_g)
    cols["norm_b"] = halves(L0_conv_out_norm_b)
    cols["b_qkv"] = tiles(L1_conv_b_qkv)
    cols["b_proj"] = tiles(L1_conv_b_proj)

    sel = np.zeros((3, 2, NST, 3, NST, P), f)
    for n in range(NST):
        sel[:, 0, n, 0, n, :] = 1
        sel[:, 0, n, 1, n, :XT] = 1
        sel[:, 1, n, 1, n, XT:] = 1
        sel[:, 1, n, 2, n, :] = 1
    sel = sel.reshape(3 * 2 * NST, 3 * NST, P).astype(ml_dtypes.bfloat16)
    onehot = np.zeros((2 * IMG, L), f)
    onehot[tok // IMG, tok] = 1
    onehot[IMG + tok % IMG, tok] = 1
    xt = np.ascontiguousarray(np.asarray(x).reshape(B, L, C).transpose(0, 2, 1))

    nc = bacc.Bacc("TRN2", target_bir_lowering=False, num_devices=1)
    arrays = {}

    def given(name, a, dtype=f):
        a = np.ascontiguousarray(a, dtype)
        arrays[name] = a
        return nc.dram_tensor(name, a.shape, mybir.dt.from_np(a.dtype), kind="ExternalInput").ap()

    x_ap = given("x_in", xt)
    mat_aps = {k: given(k + "_in", v) for k, v in mats.items()}
    col_aps = {k: given(k + "_in", v) for k, v in cols.items()}
    sel_ap = given("sel_in", sel, ml_dtypes.bfloat16)
    onehot_ap = given("onehot_in", onehot)
    out_ap = nc.dram_tensor("out_t", (B, C, L), F32, kind="ExternalOutput").ap()
    build(nc, x_ap, mat_aps, col_aps, sel_ap, onehot_ap, out_ap)
    r = run_bass_kernel_spmd(nc, [arrays], core_ids=[0])
    got = np.asarray(r.results[0]["out_t"])
    return np.ascontiguousarray(got.transpose(0, 2, 1)).reshape(B, IMG, IMG, C)
```
